# Optimizing a Trainium2 kernel written in Bass

```python
import numpy as np
import jax
import jax.numpy as jnp

def _softmax(x, axis=-1):
    return jax.nn.softmax(x, axis=axis)

def _gelu(x):
    return jax.nn.gelu(x, approximate=True)

def _silu(x):
    return jax.nn.silu(x)

def _sigmoid(x):
    return jax.nn.sigmoid(x)

def _layernorm(x, axis=-1, eps=1e-05):
    m = jnp.mean(x, axis=axis, keepdims=True)
    v = jnp.var(x, axis=axis, keepdims=True)
    return (x - m) / jnp.sqrt(v + eps)

def _scatter_add(tgt, idx, src, axis=0):
    return tgt.at[idx].add(src)

def _segment_sum(src, seg, n):
    return jax.ops.segment_sum(src, seg, n)
kernel_name = 'mk_gnn_preln_d4_gnn_r8_5f2e17'

def setup_inputs(seed: int=0):
    np.random.seed(seed)
    _w = jnp.asarray

    def _rec_inputs():
        import jax
        import jax.numpy as jnp
        _gk = jax.random.key(seed)
        x = -0.0001006 + 1 * jax.random.normal(jax.random.fold_in(_gk, 1), (12500, 48), jnp.float32)
        _s = jax.random.randint(jax.random.fold_in(_gk, 2), (200000,), 0, 12500, jnp.int32)
        _d = jax.random.randint(jax.random.fold_in(_gk, 3), (200000,), 0, 12500, jnp.int32)
        _loop = jnp.arange(12500, dtype=jnp.int32)
        src = jnp.concatenate([_s, _d, _loop])
        dst = jnp.concatenate([_d, _s, _loop])
        _o = jnp.argsort(dst, stable=True)
        src = src[_o]
        dst = dst[_o]
        edge_attr_48 = -4.21973e-05 + 0.999841 * jax.random.normal(jax.random.fold_in(_gk, 12), (412500, 48), jnp.float32)
        edge_type_8 = jax.random.randint(jax.random.fold_in(_gk, 14), (412500,), 0, 8, jnp.int32)
        edge_weight = jax.random.uniform(jax.random.fold_in(_gk, 15), (412500,), jnp.float32, 0.0, 0.999999)
        edge_weight1 = jax.random.uniform(jax.random.fold_in(_gk, 16), (412500, 1), jnp.float32, 0.0, 1)
        return (x, src, dst, edge_attr_48, edge_type_8, edge_weight, edge_weight1)
    x, src, dst, edge_attr_48, edge_type_8, edge_weight, edge_weight1 = _rec_inputs()

    def _L0_gnn_setup():
        import jax, jax.numpy as jnp
        import numpy as np
        NUM_NODES = 12500
        key = jax.random.key(seed)
        k1, k2, k3 = jax.random.split(key, 3)
        x = jax.random.normal(k1, (NUM_NODES, 48), dtype=jnp.float32)
        edge_index = jax.random.randint(k2, (2, 200000), 0, NUM_NODES, dtype=jnp.int64)
        edge_weight = jax.random.uniform(k3, (200000,), dtype=jnp.float32)
        return {'x': x, 'edge_index': edge_index, 'edge_weight': edge_weight}
    _L0_gnn_all = _L0_gnn_setup()
    _L0_gnn_in = {k: v for k, v in _L0_gnn_all.items() if k in ()}
    del _L0_gnn_all

    def _L1_gnn_setup():
        import jax, jax.numpy as jnp
        import numpy as np
        N_NODES = 12500
        N_EDGES = 200000
        D_FEAT = 48
        key = jax.random.key(seed)
        k1, k2, k3, k4 = jax.random.split(key, 4)
        node_feat = jax.random.normal(k1, (N_NODES, D_FEAT), dtype=jnp.float32)
        edge_feat = jax.random.normal(k2, (N_EDGES, D_FEAT), dtype=jnp.float32)
        src = jax.random.randint(k3, (N_EDGES,), 0, N_NODES, dtype=jnp.int32)
        dst = jax.random.randint(k4, (N_EDGES,), 0, N_NODES, dtype=jnp.int32)
        eps = jnp.zeros((1,), dtype=jnp.float32)
        return {'node_feat': node_feat, 'edge_feat': edge_feat, 'src': src, 'dst': dst, 'eps': eps}
    _L1_gnn_all = _L1_gnn_setup()
    _L1_gnn_in = {k: v for k, v in _L1_gnn_all.items() if k in ('eps',)}
    del _L1_gnn_all

    def _L2_gnn_setup():
        import jax, jax.numpy as jnp
        import numpy as np
        N_NODES = 12500
        N_EDGES = 200000
        D_IN = 48
        D_OUT = 48
        key = jax.random.key(seed)
        k1, k2, k3, k4, k5 = jax.random.split(key, 5)
        x = jax.random.normal(k1, (N_NODES, D_IN), dtype=jnp.float32)
        init_range = np.sqrt(6.0 / (D_IN + D_OUT)).astype(np.float32)
        w = jax.random.uniform(k2, (D_IN, D_OUT), dtype=jnp.float32, minval=-init_range, maxval=init_range)
        b = jnp.zeros((D_OUT,), dtype=jnp.float32)
        edge_src = jax.random.randint(k3, (N_EDGES,), 0, N_NODES, dtype=jnp.int32)
        edge_dst = jax.random.randint(k4, (N_EDGES,), 0, N_NODES, dtype=jnp.int32)
        adj_vals = jax.random.uniform(k5, (N_EDGES,), dtype=jnp.float32)
        return {'x': x, 'w': w, 'b': b, 'edge_src': edge_src, 'edge_dst': edge_dst, 'adj_vals': adj_vals}
    _L2_gnn_all = _L2_gnn_setup()
    _L2_gnn_in = {k: v for k, v in _L2_gnn_all.items() if k in ('w', 'b')}
    del _L2_gnn_all

    def _L3_gnn_setup():
        import jax, jax.numpy as jnp
        import numpy as np
        N_NODES = 6250
        N_EDGES = 200000
        IN_FEAT = 48
        OUT_FEAT = 48
        NUM_RELS = 8
        key = jax.random.key(seed)
        ks = jax.random.split(key, 9)
        s1 = float(np.sqrt(2.0) * np.sqrt(6.0 / (IN_FEAT + IN_FEAT)))
        s2 = float(np.sqrt(2.0) * np.sqrt(6.0 / (IN_FEAT + OUT_FEAT)))
        return {'inputs': jax.random.normal(ks[0], (N_NODES, IN_FEAT), dtype=jnp.float32), 'norm': jax.random.uniform(ks[1], (N_EDGES, 1), dtype=jnp.float32), 'weight1': jax.random.uniform(ks[2], (NUM_RELS, IN_FEAT, IN_FEAT), jnp.float32, -s1, s1), 'weight2': jax.random.uniform(ks[3], (NUM_RELS, IN_FEAT, OUT_FEAT), jnp.float32, -s2, s2), 'bias1': jax.random.normal(ks[4], (IN_FEAT,), dtype=jnp.float32) * 0.1, 'bias2': jax.random.normal(ks[5], (OUT_FEAT,), dtype=jnp.float32) * 0.1, 'src': jax.random.randint(ks[6], (N_EDGES,), 0, N_NODES, dtype=jnp.int64) if jax.config.jax_enable_x64 else jax.random.randint(ks[6], (N_EDGES,), 0, N_NODES).astype(jnp.int32), 'dst': jax.random.randint(ks[7], (N_EDGES,), 0, N_NODES).astype(jnp.int32), 'rel_type': jax.random.randint(ks[8], (N_EDGES,), 0, NUM_RELS).astype(jnp.int32)}
    _L3_gnn_all = _L3_gnn_setup()
    _L3_gnn_in = {k: v for k, v in _L3_gnn_all.items() if k in ('weight1', 'weight2', 'bias1', 'bias2')}
    del _L3_gnn_all
    return {'x': x, 'src': src, 'dst': dst, 'edge_attr_48': edge_attr_48, 'edge_type_8': edge_type_8, 'edge_weight': edge_weight, 'edge_weight1': edge_weight1, 'L1_gnn_eps': _L1_gnn_in['eps'], 'L2_gnn_w': _L2_gnn_in['w'], 'L2_gnn_b': _L2_gnn_in['b'], 'L3_gnn_weight1': _L3_gnn_in['weight1'], 'L3_gnn_weight2': _L3_gnn_in['weight2'], 'L3_gnn_bias1': _L3_gnn_in['bias1'], 'L3_gnn_bias2': _L3_gnn_in['bias2']}

def reference(x, src, dst, edge_attr_48, edge_type_8, edge_weight, edge_weight1, L1_gnn_eps, L2_gnn_w, L2_gnn_b, L3_gnn_weight1, L3_gnn_weight2, L3_gnn_bias1, L3_gnn_bias2):
    import jax
    import jax.numpy as jnp

    def _L0_gnn_ref(x, edge_index, edge_weight):
        import jax, jax.numpy as jnp
        import numpy as np
        NUM_NODES = 12500
        src, dst = (edge_index[0], edge_index[1])
        msgs = x[src] * edge_weight[:, None]
        out = jax.ops.segment_sum(msgs, dst, num_segments=NUM_NODES)
        return out

    def _L1_gnn_ref(node_feat, edge_feat, src, dst, eps):
        import jax, jax.numpy as jnp
        import numpy as np
        N_NODES = 12500
        N_EDGES = 200000
        D_FEAT = 48
        m = jax.nn.relu(node_feat[src] + edge_feat)
        neigh = jax.ops.segment_sum(m, dst, num_segments=N_NODES)
        return (1.0 + eps[0]) * node_feat + neigh

    def _L2_gnn_ref(x, w, b, edge_src, edge_dst, adj_vals):
        import jax, jax.numpy as jnp
        import numpy as np
        N_NODES = 12500
        N_EDGES = 200000
        D_IN = 48
        D_OUT = 48
        xw = jnp.matmul(x, w)
        msgs = adj_vals[:, None] * xw[edge_src]
        agg = jax.ops.segment_sum(msgs, edge_dst, num_segments=N_NODES)
        return jax.nn.relu(agg + b)

    def _L3_gnn_ref(inputs, norm, weight1, weight2, bias1, bias2, src, dst, rel_type):
        import jax, jax.numpy as jnp
        import numpy as np
        N_NODES = 6250
        N_EDGES = 200000
        IN_FEAT = 48
        OUT_FEAT = 48
        NUM_RELS = 8
        h1 = jax.nn.relu(jnp.einsum('ni,rij->nrj', inputs, weight1) + bias1)
        h2 = jnp.einsum('nrj,rjo->nro', h1, weight2)
        msg = h2[src, rel_type] * norm
        agg = jax.ops.segment_sum(msg, dst, num_segments=inputs.shape[0])
        return jax.nn.relu(agg + bias2)
    edge_index = jnp.stack([src, dst])
    h = jnp.maximum(_layernorm(x, axis=-1), 0.0)
    x = x + _L0_gnn_ref(h, edge_index, edge_weight)
    h = jnp.maximum(_layernorm(x, axis=-1), 0.0)
    x = x + _L1_gnn_ref(h, edge_attr_48, src, dst, L1_gnn_eps)
    h = jnp.maximum(_layernorm(x, axis=-1), 0.0)
    x = x + _L2_gnn_ref(h, L2_gnn_w, L2_gnn_b, src, dst, edge_weight)
    h = jnp.maximum(_layernorm(x, axis=-1), 0.0)
    x = x + _L3_gnn_ref(h, edge_weight1, L3_gnn_weight1, L3_gnn_weight2, L3_gnn_bias1, L3_gnn_bias2, src, dst, edge_type_8)
    return x

_drawn_inputs = setup_inputs


def setup_inputs(seed=0):
    import zlib

    import numpy as np

    out = dict(_drawn_inputs(seed))
    spreads = {'L2_gnn_b': (0.0, 2.0)}
    factors = {'L3_gnn_bias1': 5.884, 'L3_gnn_bias2': 34.916}
    for name, (base, spread) in spreads.items():
        noise = np.random.default_rng([zlib.crc32(name.encode()), seed]).standard_normal(out[name].shape)
        drawn = base * np.exp(spread * noise) if base else spread * noise
        out[name] = jnp.asarray(drawn.astype(out[name].dtype))
    for name, factor in factors.items():
        out[name] = (out[name] * factor).astype(out[name].dtype)
    return out
```

```python
import concourse.bass as bass
from concourse import mybir
from contextlib import ExitStack

F32 = mybir.dt.float32
I32 = mybir.dt.int32
ALU = mybir.AluOpType
ACT = mybir.ActivationFunctionType
AXX = mybir.AxisListType.X

N = 12500
D = 48
E = 412500
RELS = 8
LAYERS = 4
P = 128

J = 9
SB = P * J
NSB = E // SB
SLOTS = 2
ITERS = NSB // SLOTS
TAIL = E - NSB * SB
assert NSB == ITERS * SLOTS and 0 < TAIL <= P
CHUNKS = [(c, min(P, NSB - c)) for c in range(0, NSB, P)]
NC = len(CHUNKS)

W = 64
W_SHIFT = 6
MAX_WINDOWS = (N - 1) // W + 1
ACC_COLS = N + W

NP = 125
NI = N // NP
GI = 20
GROUPS = NI // GI
BANK = 512
PER_BANK = GI // 2
SPLITS = [(0, 112), (112, NP)]
LN_EPS = 1e-5

CI = 4
CN = CI * NP
NCHUNK = NI // CI
PAIRS = RELS // 2
D2 = 2 * D

B_AGG, B_EXTRA, B_GROUP, B_HT = 0, 2, 3, 7


def gnn(nc, x_in, src, dst, edge_attr, edge_type, edge_weight, edge_weight1, eps, w_l2, b_l2,
        weight1, weight2, bias1, bias2, out):
    with ExitStack() as ctx:
        def sb(name, shape, dt=F32):
            return ctx.enter_context(nc.sbuf_tensor(name, shape, dt))

        def sem(name):
            return ctx.enter_context(nc.semaphore(name))

        accbuf = sb("accbuf", [P, ACC_COLS])
        x = sb("x", [P, NI * D])
        h = sb("h", [P, NI * D])
        src_tab = sb("src_tab", [P, NSB, J], I32)
        row3_tab = sb("row3_tab", [P, NSB, J], I32)
        rel_tab = sb("rel_tab", [P, NSB, J])
        w_tab = sb("w_tab", [P, NSB, J])
        w1_tab = sb("w1_tab", [P, NSB, J])
        scratch = sb("scratch", [P, 2, NC * SB])
        onehot = sb("onehot", [P, SLOTS, J, W])
        square = onehot[:].rearrange("p q j w -> p (q j w)")[:, 0:GI * D]
        x_onehot = sb("x_onehot", [P, J, W])
        x_rel = sb("x_rel", [P, J])
        gath = sb("gath", [P, SLOTS, J, D])
        msg = sb("msg", [P, SLOTS, J, D])
        attr = sb("attr", [P, SLOTS, J, D])
        idx = sb("idx", [P, SLOTS, J], I32)
        ident = sb("ident", [P, P])
        iota_i = sb("iota_i", [P, W], I32)
        iota = sb("iota", [P, W])
        start_i = sb("start_i", [P, MAX_WINDOWS], I32)
        start = sb("start", [P, MAX_WINDOWS])
        dmin = sb("dmin", [P, NC])
        dmax = sb("dmax", [P, NC])
        win = sb("win", [1, NSB + 1, 2], I32)
        span = sb("span", [1, NSB + 1], I32)
        stat = sb("stat", [P, 4, 2, GI])
        eps1 = sb("eps1", [P, 1])
        w2m = sb("w2m", [D, D])
        bias_l2 = sb("bias_l2", [P, D])
        bias_l3 = sb("bias_l3", [P, D])
        w1s = sb("w1s", [D, RELS, D])
        w2s = sb("w2s", [D2, PAIRS, D2])
        bias_h1 = sb("bias_h1", [D2, 1])
        t_src = sb("t_src", [P, 1], I32)
        t_type = sb("t_type", [P, 1], I32)
        t_row3 = sb("t_row3", [P, 1], I32)
        t_rel = sb("t_rel", [P, 1])
        t_w = sb("t_w", [P, 1])
        t_w1 = sb("t_w1", [P, 1])
        t_dst_i = sb("t_dst_i", [1, P], I32)
        t_dst = sb("t_dst", [1, P])
        t_minmax = sb("t_minmax", [1, 3])
        t_gath = sb("t_gath", [P, D])
        t_msg = sb("t_msg", [P, D])
        t_attr = sb("t_attr", [P, D])
        t_onehot = sb("t_onehot", [P, W])

        ps = ctx.enter_context(nc.psum_tensor("ps", [P, 8, BANK], F32))

        def staged(buf, k):
            return buf[:, k * NC * SB:(k + 1) * NC * SB].rearrange("s (c e) -> s c e", c=NC)
        s_src, s_dst, s_w = (staged(accbuf, k) for k in range(3))
        s_w1, s_type = (scratch[:, k, :].rearrange("s (c e) -> s c e", c=NC) for k in range(2))
        s_src_i, s_dst_i, s_type_i = (a.bitcast(I32) for a in (s_src, s_dst, s_type))

        hT = accbuf[0:D, 0:2 * CN].rearrange("p (b n) -> p b n", b=2)
        o = 2 * CN
        h1T = accbuf[0:D2, o:o + 2 * PAIRS * CN].rearrange("p (b r n) -> p b r n", b=2, r=PAIRS)
        o += 2 * PAIRS * CN
        rows3 = accbuf[0:NP, o:o + 2 * CI * RELS * D].rearrange("p (b n) -> p b n", b=2)

        table = nc.dram_tensor("table", [N, D], F32, kind="Internal").ap()
        table3 = nc.dram_tensor("table3", [N * RELS, D], F32, kind="Internal").ap()
        table_v = table.rearrange("(p i) f -> p (i f)", p=NP)
        table3_v = table3.rearrange("(p i r) f -> p (i r f)", p=NP, r=RELS)
        x_v = x_in.rearrange("(p i) f -> p (i f)", p=NP)
        out_v = out.rearrange("(p i) f -> p (i f)", p=NP)
        attr_v = edge_attr[0:NSB * SB, :].rearrange("(s p j) f -> s p j f", p=P, j=J)

        sources = {"src": s_src_i, "dst": s_dst_i, "w": s_w, "type": s_type_i, "w1": s_w1}
        edges_in = {k: sem(f"edges_in_{k}") for k in sources}
        x_loaded, small_loaded, tail_loaded = sem("x_loaded"), sem("small_loaded"), sem("tail_loaded")
        w2_zeroed, ident_zeroed, ident_made = sem("w2_zeroed"), sem("ident_zeroed"), sem("ident_made")
        iota_made, starts_made = sem("iota_made"), sem("starts_made")
        as_float = {k: sem(f"as_float_{k}") for k in ("src", "dst", "type")}
        turned = sem("turned")
        turned_out_a, turned_out_v = sem("turned_out_a"), sem("turned_out_v")
        windows_turned, windows_out = sem("windows_turned"), sem("windows_out")
        tail_rel_turned = sem("tail_rel_turned")
        span_ready, tail_windows = sem("span_ready"), sem("tail_windows")
        windows_ready = sem("windows_ready")
        dve_chain = sem("dve_chain")
        dve_passed = sem("dve_passed")

        idx_ready = [sem(f"idx_ready{n}") for n in range(LAYERS)]
        gather_turn = [sem(f"gather_turn{n}") for n in range(LAYERS)]
        gathered = [[sem(f"gathered{n}_{q}") for q in range(SLOTS)] for n in range(LAYERS)]
        tail_gathered = [sem(f"tail_gathered{n}") for n in range(LAYERS)]
        onehot_made = [sem(f"onehot_made{n}") for n in range(LAYERS)]
        msg_made = [sem(f"msg_made{n}") for n in range(LAYERS)]
        relu_made = sem("relu_made")
        agg_done = [sem(f"agg_done{n}") for n in range(LAYERS)]
        acc_added = [sem(f"acc_added{n}") for n in range(LAYERS)]
        attr_in = [sem(f"attr_in{q}") for q in range(SLOTS)]
        layer_summed = sem("layer_summed")
        xw_shifted, xw_onehot, xw_agg, xw_added = (sem(f"xw_{k}") for k in ("shifted", "onehot", "agg", "added"))

        nodes_turned = sem("nodes_turned")
        x_updated = sem("x_updated")
        centered, squared = sem("centered"), sem("squared")
        square_used = sem("square_used")
        var_ready, dev_ready = sem("var_ready"), sem("dev_ready")
        h_ready = sem("h_ready")
        table_written = [sem(f"table_written{n}") for n in range(LAYERS)]
        hT_turned, hT_out = sem("hT_turned"), sem("hT_out")
        h1_done, h1_out = sem("h1_done"), sem("h1_out")
        rows3_done, rows3_out = sem("rows3_done"), sem("rows3_out")
        rows3_stored = [sem(f"rows3_stored{b}") for b in range(2)]
        out_ready, out_stored = sem("out_ready"), sem("out_stored")

        SMALL = 6

        JG = 3
        ORDER = ["src", "dst", "w", "w1", "type"]
        UNITS = [(k, c, j0) for k in ORDER for c in range(NC) for j0 in range(0, J, JG)]
        ACT_UNITS = 4 * NC * (J // JG)

        def unit_out(eng, u):
            if u < ACT_UNITS:
                eng.wait_ge(turned_out_a, u + 1)
            else:
                eng.wait_ge(turned_out_v, u - ACT_UNITS + 1)

        def group(buf, g):
            return buf[0:NP, g * GI * D:(g + 1) * GI * D].rearrange("p (i f) -> p i f", f=D)

        def group_psum(n):
            b = B_GROUP + 2 * (n % 2)
            return ps[0:NP, b:b + 2, 0:PER_BANK * D]

        block = ctx.enter_context(nc.Block())

        @block.sync
        def _(sp):
            def load_edges(key, flat):
                v = flat[0:NSB * SB].rearrange("(s e) -> s e", e=SB)
                for c, (s0, n) in enumerate(CHUNKS):
                    sp.dma_start(sources[key][0:n, c, :], v[s0:s0 + n, :]).then_inc(edges_in[key], 16)

            load_edges("src", src)
            for p0, p1 in SPLITS:
                sp.dma_start(x[p0:p1, :], x_v[p0:p1, :]).then_inc(x_loaded, 16)
            load_edges("dst", dst)
            load_edges("w", edge_weight)
            t0 = NSB * SB
            sp.dma_start(t_src[0:TAIL, :], src[t0:E].rearrange("(p a) -> p a", a=1)).then_inc(tail_loaded, 16)
            sp.dma_start(t_type[0:TAIL, :], edge_type[t0:E].rearrange("(p a) -> p a", a=1)).then_inc(tail_loaded, 16)
            sp.dma_start(t_w[0:TAIL, :], edge_weight[t0:E].rearrange("(p a) -> p a", a=1)).then_inc(tail_loaded, 16)
            sp.dma_start(t_w1[0:TAIL, :], edge_weight1[t0:E, :]).then_inc(tail_loaded, 16)
            sp.dma_start(t_dst_i[0:1, 0:TAIL], dst[t0:E].rearrange("(a p) -> a p", a=1)).then_inc(tail_loaded, 16)
            sp.dma_start(t_attr[0:TAIL, :], edge_attr[t0:E, :]).then_inc(tail_loaded, 16)
            load_edges("w1", edge_weight1.rearrange("e a -> (e a)"))
            load_edges("type", edge_type)
            sp.dma_start(eps1[0:NP, :], eps.rearrange("(p a) -> p a", a=1).to_broadcast([NP, 1])).then_inc(small_loaded, 16)
            sp.dma_start(w2m[:], w_l2).then_inc(small_loaded, 16)
            sp.dma_start(bias_l2[0:NP, :], b_l2.rearrange("(a f) -> a f", a=1).to_broadcast([NP, D])).then_inc(small_loaded, 16)
            sp.dma_start(bias_l3[0:NP, :], bias2.rearrange("(a f) -> a f", a=1).to_broadcast([NP, D])).then_inc(small_loaded, 16)
            sp.dma_start(w1s[:], weight1.rearrange("r i j -> i r j")).then_inc(small_loaded, 16)
            for k in range(2):
                sp.dma_start(bias_h1[k * D:(k + 1) * D, :], bias1.rearrange("(p a) -> p a", a=1)).then_inc(small_loaded, 16)
            sp.wait_ge(w2_zeroed, 1)
            w2v = weight2.rearrange("(q k) i j -> k i q j", k=2)
            for k in range(2):
                sp.dma_start(w2s[k * D:(k + 1) * D, :, k * D:(k + 1) * D], w2v[k]).then_inc(small_loaded, 16)

            def store_table(n):
                for g in range(GROUPS):
                    sp.wait_ge(h_ready, n * GROUPS + g + 1)
                    for p0, p1 in SPLITS:
                        c0, c1 = g * GI * D, (g + 1) * GI * D
                        sp.dma_start(table_v[p0:p1, c0:c1], h[p0:p1, c0:c1]).then_inc(table_written[n], 16)

            store_table(0)

            for q in range(SLOTS):
                sp.dma_start(attr[:, q], attr_v[q]).then_inc(attr_in[q], 16)
            sp.wait_ge(layer_summed, 1)
            store_table(1)
            with sp.Fori(0, ITERS - 1) as i:
                for q in range(SLOTS):
                    sp.wait_ge(msg_made[1], i * SLOTS + (q + 1))
                    s = (i + 1) * SLOTS + q
                    sp.dma_start(attr[:, q], attr_v[bass.ds(s, 1)].rearrange("s p j f -> (s p) j f")).then_inc(attr_in[q], 16)
            sp.wait_ge(layer_summed, 2)
            store_table(2)

            for c in range(NCHUNK):
                sp.wait_ge(rows3_out, (c + 1) * CI)
                w = CI * RELS * D
                for p0, p1 in SPLITS:
                    sp.dma_start(table3_v[p0:p1, c * w:(c + 1) * w], rows3[p0:p1, c % 2, :]).then_inc(rows3_stored[c % 2], 16)

            for g in range(GROUPS):
                sp.wait_ge(out_ready, g + 1)
                for p0, p1 in SPLITS:
                    c0, c1 = g * GI * D, (g + 1) * GI * D
                    sp.dma_start(out_v[p0:p1, c0:c1], x[p0:p1, c0:c1]).then_inc(out_stored, 16)
            sp.wait_ge(out_stored, 16 * GROUPS * len(SPLITS))

        @block.gpsimd
        def _(pool):
            nc.gpsimd.memset(ident[:], 0.0).then_inc(ident_zeroed, 1)
            nc.gpsimd.memset(w2s[:], 0.0).then_inc(w2_zeroed, 1)
            nc.gpsimd.iota(iota_i[:], pattern=[[1, W]], base=0, channel_multiplier=0).then_inc(iota_made, 1)
            nc.gpsimd.iota(start_i[:], pattern=[[W, MAX_WINDOWS]], base=0, channel_multiplier=0).then_inc(starts_made, 1)
            pool.wait_ge(ident_zeroed, 1)
            nc.gpsimd.affine_select(out=ident[:], in_=ident[:], compare_op=ALU.not_equal, fill=1.0, base=0,
                                    pattern=[[-1, P]], channel_multiplier=1).then_inc(ident_made, 1)

            for n in range(LAYERS):
                rows = table3 if n == 3 else table
                if n == 3:
                    for b in range(2):
                        pool.wait_ge(rows3_stored[b], 16 * len(SPLITS) * ((NCHUNK + 1 - b) // 2))
                    pool.wait_ge(turned_out_v, len(UNITS) - ACT_UNITS + 1)
                    if n > 0:
                        pool.wait_ge(msg_made[n - 1], NSB + 1)
                else:
                    pool.wait_ge(table_written[n], 16 * GROUPS * len(SPLITS))
                    if n == 0:
                        pool.wait_ge(tail_loaded, 16 * 6)
                    else:
                        pool.wait_ge(msg_made[n - 1], NSB + 1)
                t_rows = t_row3 if n == 3 else t_src
                nc.gpsimd.indirect_dma_start(
                    t_gath[0:TAIL, :], None, rows,
                    bass.IndirectOffsetOnAxis(t_rows[0:TAIL, 0:1], 0)).then_inc(tail_gathered[n], 16)
                with pool.Fori(0, ITERS) as i:
                    for q in range(SLOTS):
                        pool.wait_ge(idx_ready[n], i * SLOTS + (q + 1)).then_inc(gather_turn[n], 1)
                        for j in range(J):
                            nc.gpsimd.indirect_dma_start(
                                gath[:, q, j, :], None, rows,
                                bass.IndirectOffsetOnAxis(idx[:, q, j:j + 1], 0)).then_inc(gathered[n][q], 16)

        @block.scalar
        def _(act):
            tabs = {"src": src_tab, "dst": rel_tab, "w": w_tab, "w1": w1_tab}

            def edge_units(k0, k1):
                for u in range(k0, k1):
                    key, c, j0 = UNITS[u]
                    s0, n = CHUNKS[c]
                    act.wait_ge(turned, u + 1)
                    nc.scalar.copy(tabs[key][:, s0:s0 + n, j0:j0 + JG].rearrange("p s j -> p j s"),
                                   ps[:, B_GROUP + u % 4, 0:JG * P].rearrange("p (j s) -> p j s", j=JG)[:, :, 0:n]
                                   ).then_inc(turned_out_a, 1)

            def norm_part(n):
                for g in range(GROUPS + 1):
                    if g < GROUPS:
                        k = n * GROUPS + g
                        act.wait_ge(centered, k + 1)
                        if k > 0:
                            act.wait_ge(square_used, k)
                        nc.scalar.activation(square[0:NP, :], group(h, g).rearrange("p i f -> p (i f)"),
                                             ACT.Square).then_inc(squared, 1)
                    if g > 0:
                        k = n * GROUPS + g - 1
                        act.wait_ge(var_ready, k + 1)
                        nc.scalar.activation(stat[0:NP, 2, k % 2, :], stat[0:NP, 1, k % 2, :], ACT.Sqrt).then_inc(dev_ready, 1)

            def load_idx(n, tab, it, q):
                s = it * SLOTS + q
                v = tab[:, bass.ds(s, 1), :].rearrange("p s j -> p (s j)") if not isinstance(s, int) else tab[:, s, :]
                nc.scalar.copy(idx[:, q, :], v).then_inc(idx_ready[n], 1)

            def loop_part(n):
                tab = row3_tab if n == 3 else src_tab
                for q in range(SLOTS):
                    if n > 0:
                        act.wait_ge(gathered[n - 1][q], 16 * J * ITERS)
                    load_idx(n, tab, 0, q)
                with act.Fori(0, ITERS - 1) as i:
                    for q in range(SLOTS):
                        act.wait_ge(msg_made[n], i * SLOTS + (q + 1))
                        load_idx(n, tab, i + 1, q)
                        if n == 1:
                            nc.scalar.activation(msg[:, q], msg[:, q], ACT.Relu).then_inc(relu_made, 1)
                if n == 1:
                    for q in range(SLOTS):
                        act.wait_ge(msg_made[n], (ITERS - 1) * SLOTS + q + 1)
                        nc.scalar.activation(msg[:, q], msg[:, q], ACT.Relu).then_inc(relu_made, 1)
                    act.wait_ge(msg_made[n], NSB + 1)
                    nc.scalar.activation(t_msg[0:TAIL, :], t_msg[0:TAIL, :], ACT.Relu).then_inc(relu_made, 1)

            per = NC * (J // JG)
            edge_units(0, per)
            norm_part(0)
            edge_units(per, 3 * per)
            act.wait_ge(windows_turned, 2)
            nc.scalar.copy(win[:, 0:NSB, 0], ps[0:1, B_AGG, 0:NSB]).then_inc(windows_out, 1)
            nc.scalar.copy(span[:, 0:NSB], ps[0:1, B_AGG + 1, 0:NSB]).then_inc(windows_out, 1)
            act.wait_ge(tail_rel_turned, 1)
            nc.scalar.copy(t_rel[0:TAIL, :], ps[0:TAIL, B_EXTRA, 0:1]).then_inc(windows_out, 1)
            act.wait_ge(turned_out_a, per)
            edge_units(3 * per, 4 * per)
            loop_part(0)
            norm_part(1)
            loop_part(1)
            norm_part(2)
            loop_part(2)
            norm_part(3)
            for c in range(NCHUNK):
                for r in range(PAIRS):
                    k = c * PAIRS + r
                    act.wait_ge(h1_done, k + 1)
                    if c >= 2:
                        act.wait_ge(rows3_done, (c - 1) * CI)
                    if k == 0:
                        act.wait_ge(small_loaded, 16 * (SMALL + 3))
                    nc.scalar.activation(h1T[:, c % 2, r, :], ps[0:D2, B_GROUP + k % 2, 0:CN], ACT.Relu,
                                         bias=bias_h1[:]).then_inc(h1_out, 1)
            act.wait_ge(turned_out_v, len(UNITS) - ACT_UNITS + 1)
            loop_part(3)

        @block.vector
        def _(dve):
            chain = [0]

            def link(ins):
                chain[0] += 1
                ins.then_inc(dve_chain, 1)
                dve.wait_ge(dve_chain, chain[0])

            n_extra = dve.alloc_register("dve_extra")
            dve.reg_mov(n_extra, 0)

            def norm_a(n, g):
                k = n * GROUPS + g
                link(nc.vector.tensor_reduce(stat[0:NP, 0, k % 2, :], group(x, g), AXX, ALU.add))
                link(nc.vector.tensor_scalar(stat[0:NP, 0, k % 2, :], stat[0:NP, 0, k % 2, :], -1.0 / D, None, ALU.mult))
                nc.vector.tensor_tensor(group(h, g), group(x, g), stat[0:NP, 0, k % 2, :].unsqueeze(2).to_broadcast([NP, GI, D]),
                                        ALU.add).then_inc(centered, 1)

            def norm_b(n, g):
                k = n * GROUPS + g
                dve.wait_ge(squared, k + 1)
                nc.vector.tensor_reduce(stat[0:NP, 1, k % 2, :], square[0:NP, :].rearrange("p (i f) -> p i f", f=D),
                                        AXX, ALU.add).then_inc(square_used, 1)
                dve.wait_ge(square_used, k + 1)
                nc.vector.tensor_scalar(stat[0:NP, 1, k % 2, :], stat[0:NP, 1, k % 2, :], 1.0 / D, LN_EPS,
                                        ALU.mult, ALU.add).then_inc(var_ready, 1)

            def norm_c(n, g):
                k = n * GROUPS + g
                dve.wait_ge(dev_ready, k + 1)
                link(nc.vector.reciprocal(stat[0:NP, 3, k % 2, :], stat[0:NP, 2, k % 2, :]))
                nc.vector.scalar_tensor_tensor(
                    out=group(h, g), in0=group(h, g), scalar=0.0,
                    in1=stat[0:NP, 3, k % 2, :].unsqueeze(2).to_broadcast([NP, GI, D]),
                    op0=ALU.max, op1=ALU.mult).then_inc(h_ready, 1)

            def update_x(n, g):
                k = n * GROUPS + g
                dve.wait_ge(nodes_turned, k + 1)
                xg = group(x, g).rearrange("p (b i) f -> p b i f", b=2)
                pg = group_psum(k).rearrange("p b (i f) -> p b i f", f=D)
                if n < 2:
                    return nc.vector.tensor_tensor(xg, pg, xg, ALU.add)
                bias = (bias_l2 if n == 2 else bias_l3)[0:NP, :].unsqueeze(1).unsqueeze(1).to_broadcast([NP, 2, PER_BANK, D])
                hg = group(h, g).rearrange("p (b i) f -> p b i f", b=2)
                link(nc.vector.tensor_tensor(hg, pg, bias, ALU.add))
                return nc.vector.scalar_tensor_tensor(out=group(x, g), in0=group(h, g), scalar=0.0, in1=group(x, g),
                                                      op0=ALU.max, op1=ALU.add)

            def norm(n):
                for g in range(GROUPS + 2):
                    if g < GROUPS:
                        if n > 0:
                            u = update_x(n - 1, g)
                            u.then_inc(x_updated, 1)
                            dve.wait_ge(x_updated, (n - 1) * GROUPS + g + 1)
                        norm_a(n, g)
                    if 0 < g <= GROUPS:
                        norm_b(n, g - 1)
                    if g > 1:
                        norm_c(n, g - 2)

            def make_message(n, to, rows, weight, attrs):
                if n == 1:
                    nc.vector.tensor_tensor(to, rows, attrs, ALU.add).then_inc(msg_made[n], 1)
                else:
                    nc.vector.tensor_tensor(to, rows, weight, ALU.mult).then_inc(msg_made[n], 1)

            def further_windows(base, extra, rel, x_rel_v, x_onehot_v):
                with dve.If(extra > 0):
                    with dve.Fori(1, extra + 1) as k:
                        dve.reg_add(n_extra, n_extra, 1)
                        kk = dve.snap(k, min_val=1, max_val=MAX_WINDOWS - 1)
                        np_, nj = x_rel_v.shape[0], x_rel_v.shape[1]
                        nc.vector.tensor_scalar(x_rel_v, rel, start[0:np_, bass.ds(kk, 1)], None,
                                                ALU.subtract).then_inc(xw_shifted, 1)
                        dve.wait_ge(xw_shifted, n_extra)
                        nc.vector.tensor_tensor(x_onehot_v, iota[0:np_, :].unsqueeze(1).to_broadcast([np_, nj, W]),
                                                x_rel_v.unsqueeze(2).to_broadcast([np_, nj, W]),
                                                ALU.is_equal).then_inc(xw_onehot, 1)
                        dve.wait_ge(xw_agg, n_extra)
                        at = nc.s_assert_within(
                            base + kk * W, 0, N - 1,
                            skip_runtime_bounds_check_because="a window starts at or below the highest dst")
                        v = accbuf[0:D, bass.ds(at, W)]
                        nc.vector.tensor_tensor(v, ps[0:D, B_EXTRA, 0:W], v, ALU.add).then_inc(xw_added, 1)
                        dve.wait_ge(xw_added, n_extra).then_inc(dve_passed, 1)

            def layer(n):
                wt = w1_tab if n == 3 else w_tab
                t_wt = t_w1 if n == 3 else t_w
                link(nc.vector.memset(accbuf[0:D, :], 0.0))
                if n == 1:
                    nc.vector.scalar_tensor_tensor(out=x[0:NP, :], in0=h[0:NP, :], scalar=eps1[0:NP, 0:1],
                                                   in1=x[0:NP, :], op0=ALU.mult, op1=ALU.add).then_inc(dve_chain, 1)
                    chain[0] += 1
                with dve.Fori(0, ITERS) as i:
                    for q in range(SLOTS):
                        s = i * SLOTS + q
                        rel = rel_tab[:, bass.ds(s, 1), :].rearrange("p s j -> p (s j)")
                        nc.vector.tensor_tensor(onehot[:, q], iota[:].unsqueeze(1).to_broadcast([P, J, W]),
                                                rel.unsqueeze(2).to_broadcast([P, J, W]),
                                                ALU.is_equal).then_inc(onehot_made[n], 1)
                    for q in range(SLOTS):
                        s = i * SLOTS + q
                        dve.wait_ge(gathered[n][q], i * (16 * J) + 16 * J)
                        if n == 1:
                            dve.wait_ge(attr_in[q], i * 16 + 16)
                        wv = wt[:, bass.ds(s, 1), :].rearrange("p s j -> p (s j)").unsqueeze(2).to_broadcast([P, J, D])
                        make_message(n, msg[:, q], gath[:, q], wv, attr[:, q])
                    for q in range(SLOTS):
                        s = i * SLOTS + q
                        base = dve.value_load(win[0:1, bass.ds(s, 1), 0:1].rearrange("p s a -> p (s a)"), min_val=0, max_val=N - 1)
                        extra = dve.value_load(win[0:1, bass.ds(s, 1), 1:2].rearrange("p s a -> p (s a)"), min_val=0, max_val=MAX_WINDOWS - 1)
                        dve.wait_ge(agg_done[n], i * SLOTS + (q + 1))
                        v = accbuf[0:D, bass.ds(base, W)]
                        nc.vector.tensor_tensor(v, ps[0:D, B_AGG + q, 0:W], v, ALU.add).then_inc(acc_added[n], 1)
                        dve.wait_ge(acc_added[n], i * SLOTS + (q + 1)).then_inc(dve_passed, 1)
                        further_windows(base, extra, rel_tab[:, bass.ds(s, 1), :].rearrange("p s j -> p (s j)"),
                                        x_rel[:], x_onehot[:])
                nc.vector.tensor_tensor(t_onehot[0:TAIL, :], iota[0:TAIL, :], t_rel[0:TAIL, :].to_broadcast([TAIL, W]),
                                        ALU.is_equal).then_inc(onehot_made[n], 1)
                dve.wait_ge(tail_gathered[n], 16)
                make_message(n, t_msg[0:TAIL, :], t_gath[0:TAIL, :], t_wt[0:TAIL, :].to_broadcast([TAIL, D]),
                             t_attr[0:TAIL, :])
                base = dve.value_load(win[0:1, NSB, 0:1], min_val=0, max_val=N - 1)
                extra = dve.value_load(win[0:1, NSB, 1:2], min_val=0, max_val=MAX_WINDOWS - 1)
                dve.wait_ge(agg_done[n], NSB + 1)
                v = accbuf[0:D, bass.ds(base, W)]
                nc.vector.tensor_tensor(v, ps[0:D, B_AGG, 0:W], v, ALU.add).then_inc(acc_added[n], 1)
                dve.wait_ge(acc_added[n], NSB + 1)
                further_windows(base, extra, t_rel[0:TAIL, :], x_rel[0:TAIL, 0:1], x_onehot[0:TAIL, 0:1, :])
                dve.sem_inc(layer_summed, 1)

            for key, f, i_ in (("src", s_src, s_src_i),):
                dve.wait_ge(edges_in[key], 16 * NC)
                for c, (s0, n) in enumerate(CHUNKS):
                    nc.vector.tensor_copy(f[0:n, c, :], i_[0:n, c, :]).then_inc(as_float[key], 1)
            dve.wait_ge(x_loaded, 16 * len(SPLITS))
            norm(0)
            dve.wait_ge(iota_made, 1)
            nc.vector.tensor_copy(iota[:], iota_i[:]).then_inc(dve_chain, 1)
            dve.wait_ge(starts_made, 1)
            link(nc.vector.tensor_copy(start[:], start_i[:]))
            chain[0] += 1
            dve.wait_ge(dve_chain, chain[0])
            dve.wait_ge(edges_in["dst"], 16 * NC)
            for c, (s0, n) in enumerate(CHUNKS):
                d = s_dst[0:n, c, :]
                link(nc.vector.tensor_copy(d, s_dst_i[0:n, c, :]))
                nc.vector.tensor_reduce(dmin[0:n, c:c + 1], d, AXX, ALU.min).then_inc(dve_chain, 1)
                chain[0] += 1
                link(nc.vector.tensor_reduce(dmax[0:n, c:c + 1], d, AXX, ALU.max))
                nc.vector.tensor_tensor(dmax[0:n, c:c + 1], dmax[0:n, c:c + 1], dmin[0:n, c:c + 1],
                                        ALU.subtract).then_inc(as_float["dst"], 1)
                nc.vector.tensor_scalar(d, d, dmin[0:n, c:c + 1], None, ALU.subtract).then_inc(as_float["dst"], 1)
            dve.wait_ge(tail_loaded, 16 * 6)
            link(nc.vector.tensor_copy(t_dst[:, 0:TAIL], t_dst_i[:, 0:TAIL]))
            link(nc.vector.tensor_reduce(t_minmax[:, 0:1], t_dst[:, 0:TAIL], AXX, ALU.min))
            link(nc.vector.tensor_reduce(t_minmax[:, 1:2], t_dst[:, 0:TAIL], AXX, ALU.max))
            nc.vector.tensor_scalar(t_dst[:, 0:TAIL], t_dst[:, 0:TAIL], t_minmax[:, 0:1], None,
                                    ALU.subtract).then_inc(tail_windows, 1)
            link(nc.vector.tensor_tensor(t_minmax[:, 2:3], t_minmax[:, 1:2], t_minmax[:, 0:1], ALU.subtract))
            link(nc.vector.tensor_copy(win[:, NSB, 0:1], t_minmax[:, 0:1]))
            link(nc.vector.tensor_copy(span[:, NSB:NSB + 1], t_minmax[:, 2:3]))
            dve.wait_ge(windows_out, 3)
            nc.vector.tensor_scalar(win[:, :, 1], span[:], W_SHIFT, None, ALU.logical_shift_right).then_inc(windows_ready, 1)
            dve.wait_ge(windows_ready, 1)
            dve.wait_ge(edges_in["type"], 16 * NC)
            for c, (s0, n) in enumerate(CHUNKS):
                nc.vector.tensor_copy(s_type[0:n, c, :], s_type_i[0:n, c, :]).then_inc(as_float["type"], 1)
            dve.wait_ge(turned_out_a, NC * (J // JG))
            for u in range(ACT_UNITS, len(UNITS)):
                _, c, j0 = UNITS[u]
                s0, n = CHUNKS[c]
                dve.wait_ge(turned, u + 1)
                nc.vector.scalar_tensor_tensor(
                    out=row3_tab[:, s0:s0 + n, j0:j0 + JG].rearrange("p s j -> p j s"),
                    in0=src_tab[:, s0:s0 + n, j0:j0 + JG].rearrange("p s j -> p j s"), scalar=float(RELS),
                    in1=ps[:, B_GROUP + u % 4, 0:JG * P].rearrange("p (j s) -> p j s", j=JG)[:, :, 0:n],
                    op0=ALU.mult, op1=ALU.add).then_inc(turned_out_v, 1)
            nc.vector.scalar_tensor_tensor(out=t_row3[0:TAIL, :], in0=t_src[0:TAIL, :], scalar=float(RELS),
                                           in1=t_type[0:TAIL, :], op0=ALU.mult, op1=ALU.add).then_inc(turned_out_v, 1)
            dve.wait_ge(turned_out_a, 3 * NC * (J // JG))
            dve.wait_ge(small_loaded, 16 * (SMALL + 3))
            link(nc.vector.tensor_scalar_add(eps1[0:NP, :], eps1[0:NP, :], 1.0))

            for n in range(LAYERS):
                if n == 3:
                    for c in range(NCHUNK + 1):
                        if c < NCHUNK:
                            dve.wait_ge(hT_turned, c + 1)
                            nc.vector.tensor_copy(
                                hT[:, c % 2, :].rearrange("p (i n) -> p i n", i=CI),
                                ps[0:D, B_HT, 0:CI * P].rearrange("p (i n) -> p i n", i=CI)[:, :, 0:NP]).then_inc(hT_out, 1)
                        if c > 0:
                            cc = c - 1
                            if cc >= 2:
                                dve.wait_ge(rows3_stored[cc % 2], 16 * len(SPLITS) * (cc // 2))
                            for t in range(CI):
                                k = cc * CI + t
                                dve.wait_ge(rows3_done, k + 1)
                                w = RELS * D
                                nc.vector.tensor_copy(rows3[:, cc % 2, t * w:(t + 1) * w],
                                                      ps[0:NP, B_GROUP + 2 + k % 2, 0:w]).then_inc(rows3_out, 1)
                    for b in range(2):
                        dve.wait_ge(rows3_stored[b], 16 * len(SPLITS) * ((NCHUNK + 1 - b) // 2))
                layer(n)
                if n < 3:
                    norm(n + 1)
            for g in range(GROUPS):
                update_x(3, g).then_inc(out_ready, 1)

        @block.tensor
        def _(pe):
            n_extra = pe.alloc_register("pe_extra")
            pe.reg_mov(n_extra, 0)

            def edge_units(u0, u1):
                for u in range(u0, u1):
                    key, c, j0 = UNITS[u]
                    s0, n = CHUNKS[c]
                    v = {"src": s_src, "dst": s_dst, "w": s_w, "w1": s_w1, "type": s_type}[key]
                    v = v[0:n, c, :].rearrange("s (p j) -> s p j", j=J)
                    if u >= 4:
                        unit_out(pe, u - 4)
                    for j in range(JG):
                        last = nc.tensor.transpose(ps[:, B_GROUP + u % 4, j * P:j * P + n], v[:, :, j0 + j], ident[0:n, 0:n])
                    last.then_inc(turned, 1)

            per = NC * (J // JG)
            pe.wait_ge(ident_made, 1)
            pe.wait_ge(as_float["src"], NC)
            edge_units(0, per)
            pe.wait_ge(as_float["dst"], 2 * NC)
            edge_units(per, 2 * per)
            pe.wait_ge(edges_in["w"], 16 * NC)
            edge_units(2 * per, 3 * per)
            for b, col in ((B_AGG, dmin), (B_AGG + 1, dmax)):
                for c, (s0, n) in enumerate(CHUNKS):
                    last = nc.tensor.transpose(ps[0:1, b, s0:s0 + n], col[0:n, c:c + 1], ident[0:n, 0:n])
                last.then_inc(windows_turned, 1)
            pe.wait_ge(tail_windows, 1)
            nc.tensor.transpose(ps[0:TAIL, B_EXTRA, 0:1], t_dst[0:1, 0:TAIL], ident[0:1, 0:1]).then_inc(tail_rel_turned, 1)
            pe.wait_ge(edges_in["w1"], 16 * NC)
            edge_units(3 * per, 4 * per)
            pe.wait_ge(as_float["type"], NC)
            edge_units(4 * per, 5 * per)
            pe.wait_ge(windows_ready, 1)
            unit_out(pe, ACT_UNITS - 1)
            unit_out(pe, len(UNITS) - 1)

            def further_windows(extra, m, x_onehot_v):
                nj = x_onehot_v.shape[1]
                with pe.If(extra > 0):
                    with pe.Fori(0, extra) as k:
                        pe.reg_add(n_extra, n_extra, 1)
                        pe.wait_ge(xw_onehot, n_extra)
                        for j in range(nj):
                            last = nc.tensor.matmul(ps[0:D, B_EXTRA, 0:W], m[:, j, :], x_onehot_v[:, j, :],
                                                    start=(j == 0), stop=(j == nj - 1))
                        last.then_inc(xw_agg, 1)

            def layer(n):
                ready = relu_made if n == 1 else msg_made[n]
                with pe.Fori(0, ITERS) as i:
                    for q in range(SLOTS):
                        s = i * SLOTS + q
                        pe.wait_ge(onehot_made[n], i * SLOTS + (q + 1))
                        pe.wait_ge(ready, i * SLOTS + (q + 1))
                        for j in range(J):
                            last = nc.tensor.matmul(ps[0:D, B_AGG + q, 0:W], msg[:, q, j, :], onehot[:, q, j, :],
                                                    start=(j == 0), stop=(j == J - 1))
                        last.then_inc(agg_done[n], 1)
                        extra = pe.value_load(win[0:1, bass.ds(s, 1), 1:2].rearrange("p s a -> p (s a)"), min_val=0, max_val=MAX_WINDOWS - 1)
                        further_windows(extra, msg[:, q], x_onehot[:])
                pe.wait_ge(onehot_made[n], NSB + 1)
                pe.wait_ge(ready, NSB + 1)
                nc.tensor.matmul(ps[0:D, B_AGG, 0:W], t_msg[0:TAIL, :], t_onehot[0:TAIL, :], start=True,
                                 stop=True).then_inc(agg_done[n], 1)
                extra = pe.value_load(win[0:1, NSB, 1:2], min_val=0, max_val=MAX_WINDOWS - 1)
                further_windows(extra, t_msg[0:TAIL, :].unsqueeze(1), x_onehot[0:TAIL, 0:1, :])

            for n in range(LAYERS):
                layer(n)
                pe.wait_ge(layer_summed, n + 1)
                if n == 2:
                    pe.wait_ge(small_loaded, 16 * (SMALL + 3))
                for g in range(GROUPS):
                    k = n * GROUPS + g
                    if n == 3 and g >= 2:
                        pe.wait_ge(out_ready, g - 1)
                    elif n < 3 and k >= 2:
                        pe.wait_ge(x_updated, k - 1)
                    to = group_psum(k).rearrange("p b (i f) -> p b i f", f=D)
                    for t in range(GI):
                        v = accbuf[0:D, 0:N].rearrange("f (p i) -> f p i", i=NI)[:, :, g * GI + t]
                        to_t = to[:, t // PER_BANK, t % PER_BANK, :]
                        if n == 2:
                            last = nc.tensor.matmul(to_t, v, w2m[:], start=True, stop=True)
                        else:
                            last = nc.tensor.transpose(to_t, v, ident[0:D, 0:D])
                    last.then_inc(nodes_turned, 1)
                if n == 2:
                    def turn_h(c):
                        pe.wait_ge(h_ready, 3 * GROUPS + (c * CI) // GI + 1)
                        if c >= 1:
                            pe.wait_ge(hT_out, c)
                        for t in range(CI):
                            last = nc.tensor.transpose(ps[0:D, B_HT, t * P:t * P + NP],
                                                       h[0:NP, (c * CI + t) * D:(c * CI + t + 1) * D], ident[0:NP, 0:NP])
                        last.then_inc(hT_turned, 1)
                    pe.wait_ge(x_updated, 3 * GROUPS)
                    turn_h(0)
                    for c in range(NCHUNK):
                        pe.wait_ge(hT_out, c + 1)
                        for r in range(PAIRS):
                            k = c * PAIRS + r
                            if k >= 2:
                                pe.wait_ge(h1_out, k - 1)
                            nc.tensor.matmul(ps[0:D2, B_GROUP + k % 2, 0:CN], w1s[:, 2 * r:2 * r + 2, :].rearrange("i r j -> i (r j)"),
                                             hT[:, c % 2, :], start=True, stop=True).then_inc(h1_done, 1)
                        if c + 1 < NCHUNK:
                            turn_h(c + 1)
                        pe.wait_ge(h1_out, (c + 1) * PAIRS)
                        for t in range(CI):
                            k = c * CI + t
                            if k >= 2:
                                pe.wait_ge(rows3_out, k - 1)
                            for r in range(PAIRS):
                                last = nc.tensor.matmul(ps[0:NP, B_GROUP + 2 + k % 2, r * D2:(r + 1) * D2],
                                                        h1T[:, c % 2, r, t * NP:(t + 1) * NP], w2s[:, r, :],
                                                        start=True, stop=True)
                            last.then_inc(rows3_done, 1)


_INS = ['x', 'src', 'dst', 'edge_attr_48', 'edge_type_8', 'edge_weight', 'edge_weight1', 'L1_gnn_eps', 'L2_gnn_w',
        'L2_gnn_b', 'L3_gnn_weight1', 'L3_gnn_weight2', 'L3_gnn_bias1', 'L3_gnn_bias2']


def kernel(**inputs):
    import numpy as _np
    import concourse.bacc as _bacc
    from concourse import mybir as _mybir
    from concourse.bass_utils import run_bass_kernel_spmd as _run

    nc = _bacc.Bacc("TRN2", target_bir_lowering=False, num_devices=1)
    arrays, args = {}, []
    for name in _INS:
        a = _np.ascontiguousarray(inputs[name])
        arrays[f"in_{name}_dram"] = a
        args.append(nc.dram_tensor(f"in_{name}_dram", a.shape, _mybir.dt.from_np(a.dtype), kind="ExternalInput").ap())
    out = nc.dram_tensor("out_0_dram", (N, D), F32, kind="ExternalOutput").ap()
    gnn(nc, *args, out)
    r = _run(nc, [arrays], core_ids=[0])
    return r.results[0]["out_0_dram"]
```

```python
import concourse.bass as bass
from concourse import mybir
from contextlib import ExitStack

F32 = mybir.dt.float32
I32 = mybir.dt.int32
ALU = mybir.AluOpType
ACT = mybir.ActivationFunctionType
AXX = mybir.AxisListType.X

N = 12500
D = 48
E = 412500
RELS = 8
LAYERS = 4
P = 128

J = 9
SB = P * J
NSB = E // SB
SLOTS = 2
ITERS = NSB // SLOTS
TAIL = E - NSB * SB
assert NSB == ITERS * SLOTS and 0 < TAIL <= P
CHUNKS = [(c, min(P, NSB - c)) for c in range(0, NSB, P)]
NC = len(CHUNKS)

W = 64
W_SHIFT = 6
MAX_WINDOWS = (N - 1) // W + 1
ACC_COLS = N + W

NP = 125
NI = N // NP
GI = 20
GROUPS = NI // GI
BANK = 512
PER_BANK = GI // 2
SPLITS = [(0, 112), (112, NP)]
LN_EPS = 1e-5

CI = 4
NPAIR = CI // 2
CN = NPAIR * NP
NCHUNK = NI // CI
D2 = 2 * D
HALVES = 2
RG = RELS // 2
RH = RELS // HALVES
LAG_VAR, LAG_H = 1, 2
STATS = 4
RBUF = 4

B_AGG, B_EXTRA, B_GROUP, B_HT = 0, 2, 3, (2, 7)
IOTA_AT = BANK - W


def gnn(nc, x_in, src, dst, edge_attr, edge_type, edge_weight, edge_weight1, eps, w_l2, b_l2,
        weight1, weight2, bias1, bias2, out):
    with ExitStack() as ctx:
        def sb(name, shape, dt=F32):
            return ctx.enter_context(nc.sbuf_tensor(name, shape, dt))

        def sem(name):
            return ctx.enter_context(nc.semaphore(name))

        accbuf = sb("accbuf", [P, ACC_COLS])
        x = sb("x", [P, NI * D])
        h = sb("h", [P, NI * D])
        src_tab = sb("src_tab", [P, NSB, J], I32)
        row3_tab = sb("row3_tab", [P, NSB, J], I32)
        rel_tab = sb("rel_tab", [P, NSB, J])
        w_tab = sb("w_tab", [P, NSB, J])
        w1_tab = sb("w1_tab", [P, NSB, J])
        scratch = sb("scratch", [P, 2, NC * SB])
        onehot = sb("onehot", [P, SLOTS, J, W])
        square = onehot[:].rearrange("p q j w -> p (q j w)")[:, 0:GI * D]
        x_onehot = sb("x_onehot", [P, J, W])
        x_rel = sb("x_rel", [P, J])
        gath = sb("gath", [P, SLOTS, J, D])
        msg = sb("msg", [P, SLOTS, J, D])
        attr = sb("attr", [P, SLOTS, J, D])
        idx = sb("idx", [P, SLOTS, J], I32)
        ident = sb("ident", [P, P])
        ints = msg[:].rearrange("p q j f -> p (q j f)").bitcast(I32)
        start_i, iota_i = ints[:, 0:MAX_WINDOWS], ints[:, MAX_WINDOWS:MAX_WINDOWS + W]
        span = ints[0:1, MAX_WINDOWS + W:MAX_WINDOWS + W + NSB + 1]
        start = sb("start", [P, MAX_WINDOWS])
        dmin = sb("dmin", [P, NC])
        dmax = sb("dmax", [P, NC])
        win = sb("win", [1, NSB + 1, 2], I32)
        stat = sb("stat", [P, 4, STATS, GI])
        eps1 = sb("eps1", [P, 1])
        w2m = sb("w2m", [D, D])
        bias_l2 = sb("bias_l2", [P, D])
        bias_l3 = sb("bias_l3", [P, D])
        w1d = sb("w1d", [P, RELS, D2])
        w2d = sb("w2d", [P, RELS, D2])
        bias_h1 = sb("bias_h1", [D2, 1])
        t_src = sb("t_src", [P, 1], I32)
        t_type = sb("t_type", [P, 1], I32)
        t_row3 = sb("t_row3", [P, 1], I32)
        t_rel = sb("t_rel", [P, 1])
        t_w = sb("t_w", [P, 1])
        t_w1 = sb("t_w1", [P, 1])
        t_dst_i = sb("t_dst_i", [1, P], I32)
        t_dst = sb("t_dst", [1, P])
        t_minmax = sb("t_minmax", [1, 3])
        t_gath = sb("t_gath", [P, D])
        t_msg = sb("t_msg", [P, D])
        t_attr = sb("t_attr", [P, D])
        t_onehot = sb("t_onehot", [P, W])

        ps = ctx.enter_context(nc.psum_tensor("ps", [P, 8, BANK], F32))
        iota = ps[:, B_EXTRA, IOTA_AT:BANK]
        zero = start[:, 0:1]

        def staged(buf, k):
            return buf[:, k * NC * SB:(k + 1) * NC * SB].rearrange("s (c e) -> s c e", c=NC)
        s_src, s_dst, s_w = (staged(accbuf, k) for k in range(3))
        s_w1, s_type = (scratch[:, k, :].rearrange("s (c e) -> s c e", c=NC) for k in range(2))
        s_src_i, s_dst_i, s_type_i = (a.bitcast(I32) for a in (s_src, s_dst, s_type))

        hT = accbuf[:, 0:2 * CN].rearrange("p (b n) -> p b n", b=2)
        o = 2 * CN
        h1T = accbuf[:, o:o + 2 * RELS * CN].rearrange("p (b g n) -> p b g n", b=2, g=RG)
        o += 2 * RELS * CN
        padding = accbuf[D2:P, 0:o]
        rows3 = accbuf[0:NP, o:o + RBUF * CI * RELS * D].rearrange("p (b n) -> p b n", b=RBUF)

        table = nc.dram_tensor("table", [N, D], F32, kind="Internal").ap()
        table3 = nc.dram_tensor("table3", [N * RELS, D], F32, kind="Internal").ap()
        table_v = table.rearrange("(p i) f -> p (i f)", p=NP)
        table3_v = table3.rearrange("(p i r) f -> p (i r f)", p=NP, r=RELS)
        x_v = x_in.rearrange("(p i) f -> p (i f)", p=NP)
        out_v = out.rearrange("(p i) f -> p (i f)", p=NP)
        attr_v = edge_attr[0:NSB * SB, :].rearrange("(s p j) f -> s p j f", p=P, j=J)

        sources = {"src": s_src_i, "dst": s_dst_i, "w": s_w, "type": s_type_i, "w1": s_w1}
        edges_in = {k: sem(f"edges_in_{k}") for k in sources}
        x_loaded = [sem("x_loaded_first"), sem("x_loaded_rest")]
        small_loaded, tail_loaded = sem("small_loaded"), sem("tail_loaded")
        weights_zeroed, ident_zeroed, ident_made = sem("weights_zeroed"), sem("ident_zeroed"), sem("ident_made")
        iota_made, starts_made = sem("iota_made"), sem("starts_made")
        as_float = {k: sem(f"as_float_{k}") for k in ("src", "dst", "type")}
        consts_made = sem("consts_made")
        padding_zeroed = sem("padding_zeroed")
        acc_zeroed = sem("acc_zeroed")
        turned = sem("turned")
        turned_out_a, turned_out_v = sem("turned_out_a"), sem("turned_out_v")
        windows_turned, windows_out = sem("windows_turned"), sem("windows_out")
        tail_rel_turned = sem("tail_rel_turned")
        tail_windows = sem("tail_windows")
        windows_ready = sem("windows_ready")
        dve_chain = sem("dve_chain")
        dve_passed = sem("dve_passed")

        idx_ready = [sem(f"idx_ready{n}") for n in range(LAYERS)]
        gather_turn = [sem(f"gather_turn{n}") for n in range(LAYERS)]
        gathered = [[sem(f"gathered{n}_{q}") for q in range(SLOTS)] for n in range(LAYERS)]
        tail_gathered = [sem(f"tail_gathered{n}") for n in range(LAYERS)]
        onehot_made = [sem(f"onehot_made{n}") for n in range(LAYERS)]
        msg_made = [sem(f"msg_made{n}") for n in range(LAYERS)]
        relu_made = sem("relu_made")
        agg_done = [sem(f"agg_done{n}") for n in range(LAYERS)]
        acc_added = [sem(f"acc_added{n}") for n in range(LAYERS)]
        attr_in = [sem(f"attr_in{q}") for q in range(SLOTS)]
        layer_summed = sem("layer_summed")
        xw_shifted, xw_onehot, xw_agg, xw_added = (sem(f"xw_{k}") for k in ("shifted", "onehot", "agg", "added"))

        nodes_turned = sem("nodes_turned")
        x_updated = sem("x_updated")
        mean_ready, centered, squared = sem("mean_ready"), sem("centered"), sem("squared")
        square_used = sem("square_used")
        var_ready, dev_ready = sem("var_ready"), sem("dev_ready")
        h_ready = sem("h_ready")
        table_written = [sem(f"table_written{n}") for n in range(LAYERS)]
        hT_turned, hT_out = sem("hT_turned"), sem("hT_out")
        h1_done, h1_out = sem("h1_done"), sem("h1_out")
        rows3_done, rows3_out = sem("rows3_done"), sem("rows3_out")
        rows3_stored = [sem(f"rows3_stored{b}") for b in range(RBUF)]
        out_ready, out_stored = sem("out_ready"), sem("out_stored")

        SMALL = 10

        JG = 3
        ORDER = ["src", "dst", "w", "w1", "type"]
        UNITS = [(k, c, j0) for k in ORDER for c in range(NC) for j0 in range(0, J, JG)]
        ACT_UNITS = 4 * NC * (J // JG)

        def unit_out(eng, u):
            if u < ACT_UNITS:
                eng.wait_ge(turned_out_a, u + 1)
            else:
                eng.wait_ge(turned_out_v, u - ACT_UNITS + 1)

        def rows3_all_stored(eng):
            for b in range(RBUF):
                eng.wait_ge(rows3_stored[b], 16 * len(SPLITS) * len(range(b, NCHUNK, RBUF)))

        def group(buf, g):
            return buf[0:NP, g * GI * D:(g + 1) * GI * D].rearrange("p (i f) -> p i f", f=D)

        PER_GROUP = GI // CI

        def group_psum(n):
            b = B_GROUP + 2 * (n % 2)
            return ps[0:NP, b:b + 2, 0:PER_BANK * D]

        block = ctx.enter_context(nc.Block())

        @block.sync
        def _(sp):
            def load_edges(key, flat):
                v = flat[0:NSB * SB].rearrange("(s e) -> s e", e=SB)
                for c, (s0, n) in enumerate(CHUNKS):
                    sp.dma_start(sources[key][0:n, c, :], v[s0:s0 + n, :]).then_inc(edges_in[key], 16)

            for k, (c0, c1) in enumerate(((0, GI * D), (GI * D, NI * D))):
                for p0, p1 in SPLITS:
                    sp.dma_start(x[p0:p1, c0:c1], x_v[p0:p1, c0:c1]).then_inc(x_loaded[k], 16)
                if k == 0:
                    load_edges("src", src)
            load_edges("dst", dst)
            load_edges("w", edge_weight)
            t0 = NSB * SB
            sp.dma_start(t_src[0:TAIL, :], src[t0:E].rearrange("(p a) -> p a", a=1)).then_inc(tail_loaded, 16)
            sp.dma_start(t_type[0:TAIL, :], edge_type[t0:E].rearrange("(p a) -> p a", a=1)).then_inc(tail_loaded, 16)
            sp.dma_start(t_w[0:TAIL, :], edge_weight[t0:E].rearrange("(p a) -> p a", a=1)).then_inc(tail_loaded, 16)
            sp.dma_start(t_w1[0:TAIL, :], edge_weight1[t0:E, :]).then_inc(tail_loaded, 16)
            sp.dma_start(t_dst_i[0:1, 0:TAIL], dst[t0:E].rearrange("(a p) -> a p", a=1)).then_inc(tail_loaded, 16)
            sp.dma_start(t_attr[0:TAIL, :], edge_attr[t0:E, :]).then_inc(tail_loaded, 16)
            load_edges("w1", edge_weight1.rearrange("e a -> (e a)"))
            load_edges("type", edge_type)
            sp.dma_start(eps1[0:NP, :], eps.rearrange("(p a) -> p a", a=1).to_broadcast([NP, 1])).then_inc(small_loaded, 16)
            sp.dma_start(w2m[:], w_l2).then_inc(small_loaded, 16)
            sp.dma_start(bias_l2[0:NP, :], b_l2.rearrange("(a f) -> a f", a=1).to_broadcast([NP, D])).then_inc(small_loaded, 16)
            sp.dma_start(bias_l3[0:NP, :], bias2.rearrange("(a f) -> a f", a=1).to_broadcast([NP, D])).then_inc(small_loaded, 16)
            for k in range(2):
                sp.dma_start(bias_h1[k * D:(k + 1) * D, :], bias1.rearrange("(p a) -> p a", a=1)).then_inc(small_loaded, 16)
            sp.wait_ge(weights_zeroed, 2)
            for to, of in ((w1d, weight1), (w2d, weight2)):
                for k in range(2):
                    sp.dma_start(to[k * D:(k + 1) * D, :, k * D:(k + 1) * D],
                                 of.rearrange("r i j -> i r j")).then_inc(small_loaded, 16)

            def store_table(n):
                for g in range(GROUPS):
                    sp.wait_ge(h_ready, n * GROUPS + g + 1)
                    for p0, p1 in SPLITS:
                        c0, c1 = g * GI * D, (g + 1) * GI * D
                        sp.dma_start(table_v[p0:p1, c0:c1], h[p0:p1, c0:c1]).then_inc(table_written[n], 16)

            store_table(0)

            for q in range(SLOTS):
                sp.dma_start(attr[:, q], attr_v[q]).then_inc(attr_in[q], 16)
            sp.wait_ge(layer_summed, 1)
            store_table(1)
            with sp.Fori(0, ITERS - 1) as i:
                for q in range(SLOTS):
                    sp.wait_ge(msg_made[1], i * SLOTS + (q + 1))
                    s = (i + 1) * SLOTS + q
                    sp.dma_start(attr[:, q], attr_v[bass.ds(s, 1)].rearrange("s p j f -> (s p) j f")).then_inc(attr_in[q], 16)
            sp.wait_ge(layer_summed, 2)
            store_table(2)

            for c in range(NCHUNK):
                sp.wait_ge(rows3_out, (c + 1) * NPAIR * HALVES)
                w = CI * RELS * D
                for p0, p1 in SPLITS:
                    sp.dma_start(table3_v[p0:p1, c * w:(c + 1) * w], rows3[p0:p1, c % RBUF, :]).then_inc(rows3_stored[c % RBUF], 16)

            for g in range(GROUPS):
                sp.wait_ge(out_ready, g + 1)
                for p0, p1 in SPLITS:
                    c0, c1 = g * GI * D, (g + 1) * GI * D
                    sp.dma_start(out_v[p0:p1, c0:c1], x[p0:p1, c0:c1]).then_inc(out_stored, 16)
            sp.wait_ge(out_stored, 16 * GROUPS * len(SPLITS))

        @block.gpsimd
        def _(pool):
            nc.gpsimd.memset(ident[:], 0.0).then_inc(ident_zeroed, 1)
            nc.gpsimd.memset(w1d[:], 0.0).then_inc(weights_zeroed, 1)
            nc.gpsimd.memset(w2d[:], 0.0).then_inc(weights_zeroed, 1)
            nc.gpsimd.iota(iota_i, pattern=[[1, W]], base=0, channel_multiplier=0).then_inc(iota_made, 1)
            nc.gpsimd.iota(start_i, pattern=[[W, MAX_WINDOWS]], base=0, channel_multiplier=0).then_inc(starts_made, 1)
            pool.wait_ge(ident_zeroed, 1)
            nc.gpsimd.affine_select(out=ident[:], in_=ident[:], compare_op=ALU.not_equal, fill=1.0, base=0,
                                    pattern=[[-1, P]], channel_multiplier=1).then_inc(ident_made, 1)

            for n in range(LAYERS):
                rows = table3 if n == 3 else table
                for g in range(GROUPS):
                    k = n * GROUPS + g
                    pool.wait_ge(mean_ready, k + 1)
                    nc.gpsimd.tensor_tensor(group(h, g), group(x, g),
                                            stat[0:NP, 0, k % STATS, :].unsqueeze(2).to_broadcast([NP, GI, D]),
                                            ALU.add).then_inc(centered, 1)
                if n in (1, 2):
                    pool.wait_ge(nodes_turned, n * GROUPS)
                    nc.gpsimd.memset(accbuf[0:D, :], 0.0).then_inc(acc_zeroed, 1)
                if n == 3:
                    rows3_all_stored(pool)
                    pool.wait_ge(turned_out_v, len(UNITS) - ACT_UNITS + 1)
                    pool.wait_ge(msg_made[n - 1], NSB + 1)
                else:
                    pool.wait_ge(table_written[n], 16 * GROUPS * len(SPLITS))
                    if n == 0:
                        pool.wait_ge(tail_loaded, 16 * 6)
                    else:
                        pool.wait_ge(msg_made[n - 1], NSB + 1)
                t_rows = t_row3 if n == 3 else t_src
                nc.gpsimd.indirect_dma_start(
                    t_gath[0:TAIL, :], None, rows,
                    bass.IndirectOffsetOnAxis(t_rows[0:TAIL, 0:1], 0)).then_inc(tail_gathered[n], 16)
                with pool.Fori(0, ITERS) as i:
                    for q in range(SLOTS):
                        pool.wait_ge(idx_ready[n], i * SLOTS + (q + 1)).then_inc(gather_turn[n], 1)
                        for j in range(J):
                            nc.gpsimd.indirect_dma_start(
                                gath[:, q, j, :], None, rows,
                                bass.IndirectOffsetOnAxis(idx[:, q, j:j + 1], 0)).then_inc(gathered[n][q], 16)

        @block.scalar
        def _(act):
            tabs = {"src": src_tab, "dst": rel_tab, "w": w_tab, "w1": w1_tab}

            def edge_units(k0, k1):
                for u in range(k0, k1):
                    key, c, j0 = UNITS[u]
                    s0, n = CHUNKS[c]
                    act.wait_ge(turned, u + 1)
                    nc.scalar.copy(tabs[key][:, s0:s0 + n, j0:j0 + JG].rearrange("p s j -> p j s"),
                                   ps[:, B_GROUP + u % 4, 0:JG * P].rearrange("p (j s) -> p j s", j=JG)[:, :, 0:n]
                                   ).then_inc(turned_out_a, 1)

            def norm_step(n, t):
                if t < GROUPS:
                    k = n * GROUPS + t
                    act.wait_ge(centered, k + 1)
                    if k > 0:
                        act.wait_ge(square_used, k)
                    nc.scalar.activation(square[0:NP, :], group(h, t).rearrange("p i f -> p (i f)"),
                                         ACT.Square).then_inc(squared, 1)
                if 0 <= t - LAG_VAR < GROUPS:
                    k = n * GROUPS + t - LAG_VAR
                    act.wait_ge(var_ready, k + 1)
                    nc.scalar.activation(stat[0:NP, 2, k % STATS, :], stat[0:NP, 1, k % STATS, :],
                                         ACT.Sqrt).then_inc(dev_ready, 1)

            def norm_part(n):
                for t in range(GROUPS + LAG_VAR):
                    norm_step(n, t)

            def load_idx(n, tab, it, q):
                s = it * SLOTS + q
                v = tab[:, bass.ds(s, 1), :].rearrange("p s j -> p (s j)") if not isinstance(s, int) else tab[:, s, :]
                nc.scalar.copy(idx[:, q, :], v).then_inc(idx_ready[n], 1)

            def first_idx(n):
                tab = row3_tab if n == 3 else src_tab
                for q in range(SLOTS):
                    if n > 0:
                        act.wait_ge(gathered[n - 1][q], 16 * J * ITERS)
                    load_idx(n, tab, 0, q)

            def zero_half():
                half = ACC_COLS // 2
                nc.scalar.copy(accbuf[0:D, half:ACC_COLS],
                               zero[0:D, :].to_broadcast([D, ACC_COLS - half])).then_inc(acc_zeroed, 1)

            def loop_part(n):
                tab = row3_tab if n == 3 else src_tab
                with act.Fori(0, ITERS - 1) as i:
                    for q in range(SLOTS):
                        act.wait_ge(msg_made[n], i * SLOTS + (q + 1))
                        load_idx(n, tab, i + 1, q)
                        if n == 1:
                            nc.scalar.activation(msg[:, q], msg[:, q], ACT.Relu).then_inc(relu_made, 1)
                if n == 1:
                    for q in range(SLOTS):
                        act.wait_ge(msg_made[n], (ITERS - 1) * SLOTS + q + 1)
                        nc.scalar.activation(msg[:, q], msg[:, q], ACT.Relu).then_inc(relu_made, 1)
                    act.wait_ge(msg_made[n], NSB + 1)
                    nc.scalar.activation(t_msg[0:TAIL, :], t_msg[0:TAIL, :], ACT.Relu).then_inc(relu_made, 1)

            def float_in_place(key, f, i_):
                act.wait_ge(edges_in[key], 16 * NC)
                for c, (_, n) in enumerate(CHUNKS):
                    nc.scalar.copy(f[0:n, c, :], i_[0:n, c, :]).then_inc(as_float[key], 1)

            per = NC * (J // JG)
            float_in_place("src", s_src, s_src_i)
            for t in range(2):
                norm_step(0, t)
            edge_units(0, per)
            for t in range(2, GROUPS + LAG_VAR):
                norm_step(0, t)
            act.wait_ge(turned_out_a, per)
            first_idx(0)
            edge_units(per, 3 * per)
            act.wait_ge(windows_turned, 2)
            nc.scalar.copy(win[:, 0:NSB, 0], ps[0:1, B_AGG, 0:NSB]).then_inc(windows_out, 1)
            nc.scalar.copy(span[:, 0:NSB], ps[0:1, B_AGG + 1, 0:NSB]).then_inc(windows_out, 1)
            act.wait_ge(tail_rel_turned, 1)
            nc.scalar.copy(t_rel[0:TAIL, :], ps[0:TAIL, B_EXTRA, 0:1]).then_inc(windows_out, 1)
            act.wait_ge(turned, 3 * per)
            act.wait_ge(consts_made, 2)
            zero_half()
            loop_part(0)
            norm_part(1)
            first_idx(1)
            float_in_place("type", s_type, s_type_i)
            edge_units(3 * per, 4 * per)
            nc.scalar.copy(padding, zero[D2:P, :].to_broadcast([P - D2, padding.shape[1]])).then_inc(padding_zeroed, 1)
            loop_part(1)
            norm_part(2)
            first_idx(2)
            loop_part(2)

            def relu_chunk(c):
                for g in range(RG):
                    k = c * RG + g
                    act.wait_ge(h1_done, k + 1)
                    if c >= 2:
                        act.wait_ge(rows3_done, (c - 1) * NPAIR * HALVES)
                    nc.scalar.activation(h1T[0:D2, c % 2, g, :], ps[0:D2, B_AGG + k % 2, 0:2 * CN], ACT.Relu,
                                         bias=bias_h1[:]).then_inc(h1_out, 1)

            act.wait_ge(small_loaded, 16 * SMALL)
            for t in range(GROUPS + LAG_VAR):
                if t == GROUPS:
                    relu_chunk(0)
                norm_step(3, t)
            for c in range(1, NCHUNK):
                relu_chunk(c)
            act.wait_ge(turned_out_v, per + 1)
            first_idx(3)
            rows3_all_stored(act)
            zero_half()
            loop_part(3)

        @block.vector
        def _(dve):
            chain = [0]

            def link(ins):
                chain[0] += 1
                ins.then_inc(dve_chain, 1)
                dve.wait_ge(dve_chain, chain[0])

            n_extra = dve.alloc_register("dve_extra")
            dve.reg_mov(n_extra, 0)

            def norm_mean(n, g):
                k = n * GROUPS + g
                link(nc.vector.tensor_reduce(stat[0:NP, 0, k % STATS, :], group(x, g), AXX, ALU.add))
                nc.vector.tensor_scalar(stat[0:NP, 0, k % STATS, :], stat[0:NP, 0, k % STATS, :], -1.0 / D, None,
                                        ALU.mult).then_inc(mean_ready, 1)

            def norm_var(n, g):
                k = n * GROUPS + g
                dve.wait_ge(squared, k + 1)
                nc.vector.tensor_reduce(stat[0:NP, 1, k % STATS, :], square[0:NP, :].rearrange("p (i f) -> p i f", f=D),
                                        AXX, ALU.add).then_inc(square_used, 1)
                dve.wait_ge(square_used, k + 1)
                nc.vector.tensor_scalar(stat[0:NP, 1, k % STATS, :], stat[0:NP, 1, k % STATS, :], 1.0 / D, LN_EPS,
                                        ALU.mult, ALU.add).then_inc(var_ready, 1)

            def norm_h(n, g):
                k = n * GROUPS + g
                dve.wait_ge(dev_ready, k + 1)
                link(nc.vector.reciprocal(stat[0:NP, 3, k % STATS, :], stat[0:NP, 2, k % STATS, :]))
                nc.vector.scalar_tensor_tensor(
                    out=group(h, g), in0=group(h, g), scalar=0.0,
                    in1=stat[0:NP, 3, k % STATS, :].unsqueeze(2).to_broadcast([NP, GI, D]),
                    op0=ALU.max, op1=ALU.mult).then_inc(h_ready, 1)

            def update_x(n, g):
                k = n * GROUPS + g
                dve.wait_ge(nodes_turned, k + 1)
                xg = group(x, g).rearrange("p (b i) f -> p b i f", b=2)
                pg = group_psum(k).rearrange("p b (i f) -> p b i f", f=D)
                if n < 2:
                    return nc.vector.tensor_tensor(xg, pg, xg, ALU.add)
                bias = (bias_l2 if n == 2 else bias_l3)[0:NP, :].unsqueeze(1).unsqueeze(1).to_broadcast([NP, 2, PER_BANK, D])
                hg = group(h, g).rearrange("p (b i) f -> p b i f", b=2)
                link(nc.vector.tensor_tensor(hg, pg, bias, ALU.add))
                return nc.vector.scalar_tensor_tensor(out=group(x, g), in0=group(h, g), scalar=0.0, in1=group(x, g),
                                                      op0=ALU.max, op1=ALU.add)

            def updated(n, g):
                update_x(n, g).then_inc(x_updated, 1)
                dve.wait_ge(x_updated, n * GROUPS + g + 1)

            def norm_step(n, t):
                if t < GROUPS:
                    norm_mean(n, t)
                if 0 <= t - LAG_VAR < GROUPS:
                    norm_var(n, t - LAG_VAR)
                if 0 <= t - LAG_H < GROUPS:
                    norm_h(n, t - LAG_H)

            def norm(n):
                for t in range(GROUPS + LAG_H):
                    if n > 0 and t < GROUPS:
                        updated(n - 1, t)
                    if n == 0 and t < 2:
                        dve.wait_ge(x_loaded[t], 16 * len(SPLITS))
                    norm_step(n, t)

            def make_message(n, to, rows, weight, attrs):
                if n == 1:
                    nc.vector.tensor_tensor(to, rows, attrs, ALU.add).then_inc(msg_made[n], 1)
                else:
                    nc.vector.tensor_tensor(to, rows, weight, ALU.mult).then_inc(msg_made[n], 1)

            def further_windows(base, extra, rel, x_rel_v, x_onehot_v):
                with dve.If(extra > 0):
                    with dve.Fori(1, extra + 1) as k:
                        dve.reg_add(n_extra, n_extra, 1)
                        kk = dve.snap(k, min_val=1, max_val=MAX_WINDOWS - 1)
                        np_, nj = x_rel_v.shape[0], x_rel_v.shape[1]
                        nc.vector.tensor_scalar(x_rel_v, rel, start[0:np_, bass.ds(kk, 1)], None,
                                                ALU.subtract).then_inc(xw_shifted, 1)
                        dve.wait_ge(xw_shifted, n_extra)
                        nc.vector.tensor_tensor(x_onehot_v, iota[0:np_, :].unsqueeze(1).to_broadcast([np_, nj, W]),
                                                x_rel_v.unsqueeze(2).to_broadcast([np_, nj, W]),
                                                ALU.is_equal).then_inc(xw_onehot, 1)
                        dve.wait_ge(xw_agg, n_extra)
                        at = nc.s_assert_within(
                            base + kk * W, 0, N - 1,
                            skip_runtime_bounds_check_because="a window starts at or below the highest dst")
                        v = accbuf[0:D, bass.ds(at, W)]
                        nc.vector.tensor_tensor(v, ps[0:D, B_EXTRA, 0:W], v, ALU.add).then_inc(xw_added, 1)
                        dve.wait_ge(xw_added, n_extra).then_inc(dve_passed, 1)

            def layer(n):
                wt = w1_tab if n == 3 else w_tab
                t_wt = t_w1 if n == 3 else t_w
                if n in (0, 3):
                    if n == 0:
                        dve.wait_ge(turned, 3 * NC * (J // JG))
                    link(nc.vector.memset(accbuf[0:D, 0:ACC_COLS // 2], 0.0))
                if n == 1:
                    dve.wait_ge(h_ready, 2 * GROUPS)
                    nc.vector.scalar_tensor_tensor(out=x[0:NP, :], in0=h[0:NP, :], scalar=eps1[0:NP, 0:1],
                                                   in1=x[0:NP, :], op0=ALU.mult, op1=ALU.add).then_inc(dve_chain, 1)
                    chain[0] += 1
                    row3()
                dve.wait_ge(acc_zeroed, n + 1)
                with dve.Fori(0, ITERS) as i:
                    for q in range(SLOTS):
                        s = i * SLOTS + q
                        rel = rel_tab[:, bass.ds(s, 1), :].rearrange("p s j -> p (s j)")
                        nc.vector.tensor_tensor(onehot[:, q], iota.unsqueeze(1).to_broadcast([P, J, W]),
                                                rel.unsqueeze(2).to_broadcast([P, J, W]),
                                                ALU.is_equal).then_inc(onehot_made[n], 1)
                    for q in range(SLOTS):
                        s = i * SLOTS + q
                        dve.wait_ge(gathered[n][q], i * (16 * J) + 16 * J)
                        if n == 1:
                            dve.wait_ge(attr_in[q], i * 16 + 16)
                        wv = wt[:, bass.ds(s, 1), :].rearrange("p s j -> p (s j)").unsqueeze(2).to_broadcast([P, J, D])
                        make_message(n, msg[:, q], gath[:, q], wv, attr[:, q])
                    for q in range(SLOTS):
                        s = i * SLOTS + q
                        base = dve.value_load(win[0:1, bass.ds(s, 1), 0:1].rearrange("p s a -> p (s a)"), min_val=0, max_val=N - 1)
                        extra = dve.value_load(win[0:1, bass.ds(s, 1), 1:2].rearrange("p s a -> p (s a)"), min_val=0, max_val=MAX_WINDOWS - 1)
                        dve.wait_ge(agg_done[n], i * SLOTS + (q + 1))
                        v = accbuf[0:D, bass.ds(base, W)]
                        nc.vector.tensor_tensor(v, ps[0:D, B_AGG + q, 0:W], v, ALU.add).then_inc(acc_added[n], 1)
                        dve.wait_ge(acc_added[n], i * SLOTS + (q + 1)).then_inc(dve_passed, 1)
                        further_windows(base, extra, rel_tab[:, bass.ds(s, 1), :].rearrange("p s j -> p (s j)"),
                                        x_rel[:], x_onehot[:])
                nc.vector.tensor_tensor(t_onehot[0:TAIL, :], iota[0:TAIL, :], t_rel[0:TAIL, :].to_broadcast([TAIL, W]),
                                        ALU.is_equal).then_inc(onehot_made[n], 1)
                dve.wait_ge(tail_gathered[n], 16)
                make_message(n, t_msg[0:TAIL, :], t_gath[0:TAIL, :], t_wt[0:TAIL, :].to_broadcast([TAIL, D]),
                             t_attr[0:TAIL, :])
                base = dve.value_load(win[0:1, NSB, 0:1], min_val=0, max_val=N - 1)
                extra = dve.value_load(win[0:1, NSB, 1:2], min_val=0, max_val=MAX_WINDOWS - 1)
                dve.wait_ge(agg_done[n], NSB + 1)
                v = accbuf[0:D, bass.ds(base, W)]
                nc.vector.tensor_tensor(v, ps[0:D, B_AGG, 0:W], v, ALU.add).then_inc(acc_added[n], 1)
                dve.wait_ge(acc_added[n], NSB + 1)
                further_windows(base, extra, t_rel[0:TAIL, :], x_rel[0:TAIL, 0:1], x_onehot[0:TAIL, 0:1, :])
                dve.sem_inc(layer_summed, 1)

            def row3():
                dve.wait_ge(turned_out_a, NC * (J // JG))
                for u in range(ACT_UNITS, len(UNITS)):
                    _, c, j0 = UNITS[u]
                    s0, n = CHUNKS[c]
                    dve.wait_ge(turned, u + 1)
                    nc.vector.scalar_tensor_tensor(
                        out=row3_tab[:, s0:s0 + n, j0:j0 + JG].rearrange("p s j -> p j s"),
                        in0=src_tab[:, s0:s0 + n, j0:j0 + JG].rearrange("p s j -> p j s"), scalar=float(RELS),
                        in1=ps[:, B_GROUP + u % 4, 0:JG * P].rearrange("p (j s) -> p j s", j=JG)[:, :, 0:n],
                        op0=ALU.mult, op1=ALU.add).then_inc(turned_out_v, 1)
                nc.vector.scalar_tensor_tensor(out=t_row3[0:TAIL, :], in0=t_src[0:TAIL, :], scalar=float(RELS),
                                               in1=t_type[0:TAIL, :], op0=ALU.mult, op1=ALU.add).then_inc(turned_out_v, 1)

            dve.wait_ge(iota_made, 1)
            nc.vector.tensor_copy(iota, iota_i).then_inc(consts_made, 1)
            dve.wait_ge(starts_made, 1)
            nc.vector.tensor_copy(start[:], start_i).then_inc(consts_made, 1)
            norm(0)
            dve.wait_ge(consts_made, 2)
            dve.wait_ge(edges_in["dst"], 16 * NC)
            for c, (s0, n) in enumerate(CHUNKS):
                d = s_dst_i[0:n, c, :]
                nc.vector.tensor_reduce(dmin[0:n, c:c + 1], d, AXX, ALU.min).then_inc(dve_chain, 1)
                chain[0] += 1
                link(nc.vector.tensor_reduce(dmax[0:n, c:c + 1], d, AXX, ALU.max))
                nc.vector.tensor_tensor(dmax[0:n, c:c + 1], dmax[0:n, c:c + 1], dmin[0:n, c:c + 1],
                                        ALU.subtract).then_inc(as_float["dst"], 1)
                nc.vector.tensor_scalar(s_dst[0:n, c, :], d, dmin[0:n, c:c + 1], None,
                                        ALU.subtract).then_inc(as_float["dst"], 1)
            dve.wait_ge(tail_loaded, 16 * 6)
            link(nc.vector.tensor_copy(t_dst[:, 0:TAIL], t_dst_i[:, 0:TAIL]))
            link(nc.vector.tensor_reduce(t_minmax[:, 0:1], t_dst[:, 0:TAIL], AXX, ALU.min))
            link(nc.vector.tensor_reduce(t_minmax[:, 1:2], t_dst[:, 0:TAIL], AXX, ALU.max))
            nc.vector.tensor_scalar(t_dst[:, 0:TAIL], t_dst[:, 0:TAIL], t_minmax[:, 0:1], None,
                                    ALU.subtract).then_inc(tail_windows, 1)
            link(nc.vector.tensor_tensor(t_minmax[:, 2:3], t_minmax[:, 1:2], t_minmax[:, 0:1], ALU.subtract))
            link(nc.vector.tensor_copy(win[:, NSB, 0:1], t_minmax[:, 0:1]))
            link(nc.vector.tensor_copy(span[:, NSB:NSB + 1], t_minmax[:, 2:3]))
            dve.wait_ge(windows_out, 3)
            nc.vector.tensor_scalar(win[:, :, 1], span, W_SHIFT, None, ALU.logical_shift_right).then_inc(windows_ready, 1)
            dve.wait_ge(windows_ready, 1)
            dve.wait_ge(turned_out_a, 3 * NC * (J // JG))
            dve.wait_ge(small_loaded, 16 * SMALL)
            link(nc.vector.tensor_scalar_add(eps1[0:NP, :], eps1[0:NP, :], 1.0))

            def turn_out_h(c):
                dve.wait_ge(hT_turned, c + 1)
                if c >= 2:
                    dve.wait_ge(h1_done, (c - 1) * RG)
                nc.vector.tensor_copy(
                    hT[0:D2, c % 2, :].rearrange("p (t n) -> p t n", t=NPAIR),
                    ps[0:D2, B_HT[c % 2], 0:NPAIR * P].rearrange("p (t n) -> p t n", t=NPAIR)[:, :, 0:NP]).then_inc(hT_out, 1)

            def rows_chunk(c):
                if c >= RBUF:
                    dve.wait_ge(rows3_stored[c % RBUF], 16 * len(SPLITS) * (c // RBUF))
                for t in range(NPAIR):
                    for half in range(HALVES):
                        k = (c * NPAIR + t) * HALVES + half
                        dve.wait_ge(rows3_done, k + 1)
                        to = rows3[:, c % RBUF, 2 * t * RELS * D:2 * (t + 1) * RELS * D].rearrange(
                            "p (a r f) -> p a r f", a=2, r=RELS)[:, :, half * RH:(half + 1) * RH, :]
                        of = ps[0:NP, B_GROUP + k % 4, 0:RH * D2].rearrange("p (r a f) -> p a r f", r=RH, a=2)
                        nc.vector.tensor_copy(to, of).then_inc(rows3_out, 1)
                    if t == 0 and c + 2 < NCHUNK:
                        turn_out_h(c + 2)

            for n in range(LAYERS):
                if n == 3:
                    for t in range(GROUPS + LAG_H):
                        if t < GROUPS:
                            updated(2, t)
                        if t == GROUPS - 1:
                            turn_out_h(0)
                            turn_out_h(1)
                        norm_step(3, t)
                    for c in range(NCHUNK):
                        rows_chunk(c)
                    rows3_all_stored(dve)
                layer(n)
                if n < 2:
                    norm(n + 1)
            for g in range(GROUPS):
                update_x(3, g).then_inc(out_ready, 1)

        @block.tensor
        def _(pe):
            n_extra = pe.alloc_register("pe_extra")
            pe.reg_mov(n_extra, 0)

            def edge_units(u0, u1):
                for u in range(u0, u1):
                    key, c, j0 = UNITS[u]
                    s0, n = CHUNKS[c]
                    v = {"src": s_src, "dst": s_dst, "w": s_w, "w1": s_w1, "type": s_type}[key]
                    v = v[0:n, c, :].rearrange("s (p j) -> s p j", j=J)
                    if u >= 4:
                        unit_out(pe, u - 4)
                    for j in range(JG):
                        last = nc.tensor.transpose(ps[:, B_GROUP + u % 4, j * P:j * P + n], v[:, :, j0 + j], ident[0:n, 0:n])
                    last.then_inc(turned, 1)

            per = NC * (J // JG)
            pe.wait_ge(ident_made, 1)
            pe.wait_ge(as_float["src"], NC)
            edge_units(0, per)
            pe.wait_ge(as_float["dst"], 2 * NC)
            edge_units(per, 2 * per)
            pe.wait_ge(edges_in["w"], 16 * NC)
            edge_units(2 * per, 3 * per)
            for b, col in ((B_AGG, dmin), (B_AGG + 1, dmax)):
                for c, (s0, n) in enumerate(CHUNKS):
                    last = nc.tensor.transpose(ps[0:1, b, s0:s0 + n], col[0:n, c:c + 1], ident[0:n, 0:n])
                last.then_inc(windows_turned, 1)
            pe.wait_ge(tail_windows, 1)
            nc.tensor.transpose(ps[0:TAIL, B_EXTRA, 0:1], t_dst[0:1, 0:TAIL], ident[0:1, 0:1]).then_inc(tail_rel_turned, 1)
            pe.wait_ge(windows_ready, 1)
            unit_out(pe, 3 * per - 1)

            def further_windows(extra, m, x_onehot_v):
                nj = x_onehot_v.shape[1]
                with pe.If(extra > 0):
                    with pe.Fori(0, extra) as k:
                        pe.reg_add(n_extra, n_extra, 1)
                        pe.wait_ge(xw_onehot, n_extra)
                        for j in range(nj):
                            last = nc.tensor.matmul(ps[0:D, B_EXTRA, 0:W], m[:, j, :], x_onehot_v[:, j, :],
                                                    start=(j == 0), stop=(j == nj - 1))
                        last.then_inc(xw_agg, 1)

            def layer(n):
                ready = relu_made if n == 1 else msg_made[n]
                with pe.Fori(0, ITERS) as i:
                    for q in range(SLOTS):
                        s = i * SLOTS + q
                        pe.wait_ge(onehot_made[n], i * SLOTS + (q + 1))
                        pe.wait_ge(ready, i * SLOTS + (q + 1))
                        for j in range(J):
                            last = nc.tensor.matmul(ps[0:D, B_AGG + q, 0:W], msg[:, q, j, :], onehot[:, q, j, :],
                                                    start=(j == 0), stop=(j == J - 1))
                        last.then_inc(agg_done[n], 1)
                        extra = pe.value_load(win[0:1, bass.ds(s, 1), 1:2].rearrange("p s a -> p (s a)"), min_val=0, max_val=MAX_WINDOWS - 1)
                        further_windows(extra, msg[:, q], x_onehot[:])
                pe.wait_ge(onehot_made[n], NSB + 1)
                pe.wait_ge(ready, NSB + 1)
                nc.tensor.matmul(ps[0:D, B_AGG, 0:W], t_msg[0:TAIL, :], t_onehot[0:TAIL, :], start=True,
                                 stop=True).then_inc(agg_done[n], 1)
                extra = pe.value_load(win[0:1, NSB, 1:2], min_val=0, max_val=MAX_WINDOWS - 1)
                further_windows(extra, t_msg[0:TAIL, :].unsqueeze(1), x_onehot[0:TAIL, 0:1, :])

            for n in range(LAYERS):
                if n == 1:
                    pe.wait_ge(x_updated, GROUPS)
                    pe.wait_ge(edges_in["w1"], 16 * NC)
                    edge_units(3 * per, 4 * per)
                    pe.wait_ge(as_float["type"], NC)
                    edge_units(4 * per, 5 * per)
                    unit_out(pe, ACT_UNITS - 1)
                    unit_out(pe, len(UNITS) - 1)
                layer(n)
                pe.wait_ge(layer_summed, n + 1)
                if n == 2:
                    pe.wait_ge(small_loaded, 16 * SMALL)
                for g in range(GROUPS):
                    k = n * GROUPS + g
                    if n == 3 and g >= 2:
                        pe.wait_ge(out_ready, g - 1)
                    elif n < 3 and k >= 2:
                        pe.wait_ge(x_updated, k - 1)
                    to = group_psum(k).rearrange("p b (i f) -> p b i f", f=D)
                    for t in range(GI):
                        v = accbuf[0:D, 0:N].rearrange("f (p i) -> f p i", i=NI)[:, :, g * GI + t]
                        to_t = to[:, t // PER_BANK, t % PER_BANK, :]
                        if n == 2:
                            last = nc.tensor.matmul(to_t, v, w2m[:], start=True, stop=True)
                        else:
                            last = nc.tensor.transpose(to_t, v, ident[0:D, 0:D])
                    last.then_inc(nodes_turned, 1)
                if n == 2:
                    def turn_h(c):
                        pe.wait_ge(h_ready, 3 * GROUPS + c // PER_GROUP + 1)
                        if c >= 2:
                            pe.wait_ge(hT_out, c - 1)
                        for t in range(NPAIR):
                            at = (c * CI + 2 * t) * D
                            last = nc.tensor.transpose(ps[0:D2, B_HT[c % 2], t * P:t * P + NP], h[0:NP, at:at + D2],
                                                       ident[0:NP, 0:NP])
                        last.then_inc(hT_turned, 1)

                    def products(c, g):
                        k = c * RG + g
                        pe.wait_ge(hT_out, c + 1)
                        if k >= 2:
                            pe.wait_ge(h1_out, k - 1)
                        for r in range(2):
                            last = nc.tensor.matmul(ps[0:D2, B_AGG + k % 2, r * CN:(r + 1) * CN], w1d[:, 2 * g + r, :],
                                                    hT[:, c % 2, :], start=True, stop=True)
                        last.then_inc(h1_done, 1)

                    def rows_of_pair(c, t, half):
                        k = (c * NPAIR + t) * HALVES + half
                        pe.wait_ge(h1_out, c * RG + (half + 1) * RG // HALVES)
                        if k >= 4:
                            pe.wait_ge(rows3_out, k - 3)
                        for r in range(RH):
                            rel = half * RH + r
                            at = (rel % 2) * CN + t * NP
                            last = nc.tensor.matmul(ps[0:NP, B_GROUP + k % 4, r * D2:(r + 1) * D2],
                                                    h1T[:, c % 2, rel // 2, at:at + NP], w2d[:, rel, :],
                                                    start=True, stop=True)
                        last.then_inc(rows3_done, 1)

                    pe.wait_ge(padding_zeroed, 1)
                    turn_h(0)
                    turn_h(1)
                    for g in range(RG):
                        products(0, g)
                    pe.wait_ge(x_updated, 3 * GROUPS)
                    for c in range(NCHUNK):
                        for g in range(RG):
                            if c + 1 < NCHUNK:
                                products(c + 1, g)
                            rows_of_pair(c, g // HALVES, g % HALVES)
                            if g == 1 and c + 2 < NCHUNK:
                                turn_h(c + 2)


_INS = ['x', 'src', 'dst', 'edge_attr_48', 'edge_type_8', 'edge_weight', 'edge_weight1', 'L1_gnn_eps', 'L2_gnn_w',
        'L2_gnn_b', 'L3_gnn_weight1', 'L3_gnn_weight2', 'L3_gnn_bias1', 'L3_gnn_bias2']


def kernel(**inputs):
    import numpy as _np
    import concourse.bacc as _bacc
    from concourse import mybir as _mybir
    from concourse.bass_utils import run_bass_kernel_spmd as _run

    nc = _bacc.Bacc("TRN2", target_bir_lowering=False, num_devices=1)
    arrays, args = {}, []
    for name in _INS:
        a = _np.ascontiguousarray(inputs[name])
        arrays[f"in_{name}_dram"] = a
        args.append(nc.dram_tensor(f"in_{name}_dram", a.shape, _mybir.dt.from_np(a.dtype), kind="ExternalInput").ap())
    out = nc.dram_tensor("out_0_dram", (N, D), F32, kind="ExternalOutput").ap()
    gnn(nc, *args, out)
    r = _run(nc, [arrays], core_ids=[0])
    return r.results[0]["out_0_dram"]
```
